# Optimizing a Trainium2 kernel written in Bass

```python
import numpy as np
import jax
import jax.numpy as jnp

def _softmax(x, axis=-1):
    return jax.nn.softmax(x, axis=axis)

def _gelu(x):
    return jax.nn.gelu(x, approximate=True)

def _silu(x):
    return jax.nn.silu(x)

def _sigmoid(x):
    return jax.nn.sigmoid(x)

def _layernorm(x, axis=-1, eps=1e-05):
    m = jnp.mean(x, axis=axis, keepdims=True)
    v = jnp.var(x, axis=axis, keepdims=True)
    return (x - m) / jnp.sqrt(v + eps)

def _scatter_add(tgt, idx, src, axis=0):
    return tgt.at[idx].add(src)

def _segment_sum(src, seg, n):
    return jax.ops.segment_sum(src, seg, n)
kernel_name = 'mk_audio_tower_d1_tok_audfeat1024_r4_b118d9'

def setup_inputs(seed: int=0):
    np.random.seed(seed)
    _w = jnp.asarray

    def _rec_inputs():
        import jax
        import jax.numpy as jnp
        _rk = jax.random.key(seed)
        x = -0.000123307 + 1.00004 * jax.random.normal(jax.random.fold_in(_rk, 1), (64, 80, 125), jnp.float32)
        return x
    x = _rec_inputs()

    def _L0_tok_setup():
        import jax, jax.numpy as jnp
        import numpy as np
        N_MELS = 80
        PATCH_FRAMES = 8
        HOP_FRAMES = 4
        D_MODEL = 256
        PATCH_DIM = N_MELS * PATCH_FRAMES

        def _patchify(mel):
            T = mel.shape[2]
            N = (T - PATCH_FRAMES) // HOP_FRAMES + 1
            idx = jnp.arange(N)[:, None] * HOP_FRAMES + jnp.arange(PATCH_FRAMES)[None, :]
            patches = mel[:, :, idx]
            patches = jnp.transpose(patches, (0, 2, 1, 3))
            return patches.reshape(patches.shape[0], N, PATCH_DIM)
        key = jax.random.key(seed)
        k1, k2, k3 = jax.random.split(key, 3)
        B, T = (32, 1024)
        mel = jax.random.normal(k1, (B, N_MELS, T), dtype=jnp.float32)
        bound = 1.0 / np.sqrt(PATCH_DIM)
        W = jax.random.uniform(k2, (PATCH_DIM, D_MODEL), dtype=jnp.float32, minval=-bound, maxval=bound)
        b = jax.random.uniform(k3, (D_MODEL,), dtype=jnp.float32, minval=-bound, maxval=bound)
        gamma = jnp.ones((D_MODEL,), dtype=jnp.float32)
        beta = jnp.zeros((D_MODEL,), dtype=jnp.float32)
        return {'mel': mel, 'W': W, 'b': b, 'gamma': gamma, 'beta': beta}
    _L0_tok_all = _L0_tok_setup()
    _L0_tok_in = {k: v for k, v in _L0_tok_all.items() if k in ('W', 'b', 'gamma', 'beta')}
    del _L0_tok_all

    def _L0_attn_setup():
        import jax, jax.numpy as jnp
        import numpy as np
        B, S, H, NH = (2, 512, 256, 16)
        HD = H // NH
        SCALE = HD ** (-0.5)
        EPS = 1e-05

        def _weight_quant(w):
            scale = 1.0 / jnp.clip(jnp.mean(jnp.abs(w)), 1e-05)
            wq = jnp.clip(jnp.round(w * scale), -1.0, 1.0) / scale
            return w + jax.lax.stop_gradient(wq - w)

        def _act_quant(x):
            scale = 127.0 / jnp.clip(jnp.max(jnp.abs(x), axis=-1, keepdims=True), 1e-05)
            y = jnp.clip(jnp.round(x * scale), -128.0, 127.0) / scale
            return x + jax.lax.stop_gradient(y - x)

        def _bitlinear(x, w):
            mu = jnp.mean(x, axis=(1, 2), keepdims=True)
            var = jnp.var(x, axis=(1, 2), keepdims=True)
            x_norm = (x - mu) * jax.lax.rsqrt(var + EPS)
            return _act_quant(x_norm) @ _weight_quant(w).T
        key = jax.random.key(seed)
        kx, k1, k2, k3, k4 = jax.random.split(key, 5)
        x = jax.random.normal(kx, (B, S, H), dtype=jnp.float32)
        init = 0.02
        w_q = jax.random.normal(k1, (H, H), dtype=jnp.float32) * init
        w_k = jax.random.normal(k2, (H, H), dtype=jnp.float32) * init
        w_v = jax.random.normal(k3, (H, H), dtype=jnp.float32) * init
        w_o = jax.random.normal(k4, (H, H), dtype=jnp.float32) * init
        return {'x': x, 'w_q': w_q, 'w_k': w_k, 'w_v': w_v, 'w_o': w_o}
    _L0_attn_all = _L0_attn_setup()
    _L0_attn_in = {k: v for k, v in _L0_attn_all.items() if k in ('w_q', 'w_k', 'w_v', 'w_o')}
    del _L0_attn_all

    def _L0_ffn_setup():
        import jax, jax.numpy as jnp
        import numpy as np
        D, H, O, E, TOPK = (256, 1024, 256, 8, 2)
        B, L = (2, 512)
        ROUTE_SCALE = 1.0
        key = jax.random.key(seed)
        ks = jax.random.split(key, 7)
        gb = float(np.sqrt(6.0 / (E + D)))
        return {'x': jax.random.normal(ks[0], (B, L, D), dtype=jnp.float32), 'gate_w': jax.random.uniform(ks[1], (E, D), jnp.float32, -gb, gb), 'gate_b': jnp.zeros((E,), jnp.float32), 'w1': jax.random.normal(ks[2], (E, D, H), jnp.float32) * 0.02, 'b1': jnp.zeros((E, H), jnp.float32), 'w2': jax.random.normal(ks[3], (E, H, O), jnp.float32) * 0.02, 'b2': jnp.zeros((E, O), jnp.float32)}
    _L0_ffn_all = _L0_ffn_setup()
    _L0_ffn_in = {k: v for k, v in _L0_ffn_all.items() if k in ('gate_w', 'gate_b', 'w1', 'b1', 'w2', 'b2')}
    del _L0_ffn_all
    return {'x': x, 'L0_tok_W': _L0_tok_in['W'], 'L0_tok_b': _L0_tok_in['b'], 'L0_tok_gamma': _L0_tok_in['gamma'], 'L0_tok_beta': _L0_tok_in['beta'], 'L0_attn_w_q': _L0_attn_in['w_q'], 'L0_attn_w_k': _L0_attn_in['w_k'], 'L0_attn_w_v': _L0_attn_in['w_v'], 'L0_attn_w_o': _L0_attn_in['w_o'], 'L0_ffn_gate_w': _L0_ffn_in['gate_w'], 'L0_ffn_gate_b': _L0_ffn_in['gate_b'], 'L0_ffn_w1': _L0_ffn_in['w1'], 'L0_ffn_b1': _L0_ffn_in['b1'], 'L0_ffn_w2': _L0_ffn_in['w2'], 'L0_ffn_b2': _L0_ffn_in['b2']}

def reference(x, L0_tok_W, L0_tok_b, L0_tok_gamma, L0_tok_beta, L0_attn_w_q, L0_attn_w_k, L0_attn_w_v, L0_attn_w_o, L0_ffn_gate_w, L0_ffn_gate_b, L0_ffn_w1, L0_ffn_b1, L0_ffn_w2, L0_ffn_b2):
    import jax
    import jax.numpy as jnp

    def _L0_tok_ref(mel, W, b, gamma, beta):
        import jax, jax.numpy as jnp
        import numpy as np
        N_MELS = 80
        PATCH_FRAMES = 8
        HOP_FRAMES = 4
        D_MODEL = 256
        PATCH_DIM = N_MELS * PATCH_FRAMES

        def _patchify(mel):
            T = mel.shape[2]
            N = (T - PATCH_FRAMES) // HOP_FRAMES + 1
            idx = jnp.arange(N)[:, None] * HOP_FRAMES + jnp.arange(PATCH_FRAMES)[None, :]
            patches = mel[:, :, idx]
            patches = jnp.transpose(patches, (0, 2, 1, 3))
            return patches.reshape(patches.shape[0], N, PATCH_DIM)
        patches = _patchify(mel)
        x = jnp.einsum('bnp,pd->bnd', patches, W) + b
        mu = jnp.mean(x, axis=-1, keepdims=True)
        var = jnp.mean(jnp.square(x - mu), axis=-1, keepdims=True)
        x_hat = (x - mu) * jax.lax.rsqrt(var + 1e-05)
        return x_hat * gamma + beta

    def _L0_attn_ref(x, w_q, w_k, w_v, w_o):
        import jax, jax.numpy as jnp
        import numpy as np
        B, S, H, NH = (2, 512, 256, 16)
        HD = H // NH
        SCALE = HD ** (-0.5)
        EPS = 1e-05

        def _weight_quant(w):
            scale = 1.0 / jnp.clip(jnp.mean(jnp.abs(w)), 1e-05)
            wq = jnp.clip(jnp.round(w * scale), -1.0, 1.0) / scale
            return w + jax.lax.stop_gradient(wq - w)

        def _act_quant(x):
            scale = 127.0 / jnp.clip(jnp.max(jnp.abs(x), axis=-1, keepdims=True), 1e-05)
            y = jnp.clip(jnp.round(x * scale), -128.0, 127.0) / scale
            return x + jax.lax.stop_gradient(y - x)

        def _bitlinear(x, w):
            mu = jnp.mean(x, axis=(1, 2), keepdims=True)
            var = jnp.var(x, axis=(1, 2), keepdims=True)
            x_norm = (x - mu) * jax.lax.rsqrt(var + EPS)
            return _act_quant(x_norm) @ _weight_quant(w).T
        bsz, seq_len, hidden = x.shape
        q = _bitlinear(x, w_q).reshape(bsz, seq_len, NH, HD).transpose(0, 2, 1, 3)
        k = _bitlinear(x, w_k).reshape(bsz, seq_len, NH, HD).transpose(0, 2, 1, 3)
        v = _bitlinear(x, w_v).reshape(bsz, seq_len, NH, HD).transpose(0, 2, 1, 3)
        scores = jnp.einsum('bhqd,bhkd->bhqk', q, k) * SCALE
        attn = jax.nn.softmax(scores, axis=-1)
        out = jnp.einsum('bhqk,bhkd->bhqd', attn, v)
        out = out.transpose(0, 2, 1, 3).reshape(bsz, seq_len, hidden)
        return _bitlinear(out, w_o)

    def _L0_ffn_ref(x, gate_w, gate_b, w1, b1, w2, b2):
        import jax, jax.numpy as jnp
        import numpy as np
        D, H, O, E, TOPK = (256, 1024, 256, 8, 2)
        B, L = (2, 512)
        ROUTE_SCALE = 1.0
        Bb, Ll, Dd = x.shape
        N = Bb * Ll
        x_flat = x.reshape(N, Dd)
        logits = x_flat @ gate_w.T + gate_b
        probs = jax.nn.softmax(logits * ROUTE_SCALE, axis=-1)
        topk_vals, topk_idx = jax.lax.top_k(probs, TOPK)
        dense_gate = jnp.zeros((N, E), probs.dtype).at[jnp.arange(N)[:, None], topk_idx].set(topk_vals)
        h = jax.nn.relu(jnp.einsum('nd,edh->neh', x_flat, w1) + b1)
        y = jnp.einsum('neh,eho->neo', h, w2) + b2
        out_flat = jnp.einsum('ne,neo->no', dense_gate, y)
        return out_flat.reshape(Bb, Ll, O)
    h = _L0_tok_ref(x, L0_tok_W, L0_tok_b, L0_tok_gamma, L0_tok_beta)
    h = h + _L0_attn_ref(_layernorm(h, axis=-1), L0_attn_w_q, L0_attn_w_k, L0_attn_w_v, L0_attn_w_o)
    h = h + _L0_ffn_ref(_layernorm(h, axis=-1), L0_ffn_gate_w, L0_ffn_gate_b, L0_ffn_w1, L0_ffn_b1, L0_ffn_w2, L0_ffn_b2)
    return h

_drawn_inputs = setup_inputs


def setup_inputs(seed=0):
    import zlib

    import numpy as np

    out = dict(_drawn_inputs(seed))
    spreads = {'L0_tok_gamma': (1.0, 0.2),
     'L0_tok_beta': (0.0, 0.1),
     'L0_ffn_gate_b': (0.0, 0.567),
     'L0_ffn_b1': (0.0, 0.324),
     'L0_ffn_b2': (0.0, 0.1)}
    factors = {'L0_attn_w_q': 5.537, 'L0_attn_w_k': 5.336}
    for name, (base, spread) in spreads.items():
        noise = np.random.default_rng([zlib.crc32(name.encode()), seed]).standard_normal(out[name].shape)
        drawn = base * np.exp(spread * noise) if base else spread * noise
        out[name] = jnp.asarray(drawn.astype(out[name].dtype))
    for name, factor in factors.items():
        out[name] = (out[name] * factor).astype(out[name].dtype)
    return out
```

```python
from contextlib import ExitStack, contextmanager

import numpy as np
import concourse.bass as bass
from concourse import mybir

B, MELS, FRAMES = 64, 80, 125
PF, HOP, NP = 8, 4, 30
D, NH, HD = 256, 16, 16
E, FF = 8, 1024
P = 128
PADN = 32
BPT = P // PADN
TILES = B // BPT
KC = D // P
HC = FF // P
G, GH = 4, 4
GD = GH * HD
SLOT_TILES = B * NP * 2 // P + E - 1
SLOTS = SLOT_TILES * P
SPARE = SLOTS + 2 * TILES * P
EPS = 1e-5
MAGIC = 1.5 * 2.0 ** 23

C_IDENT, C_MEAN, C_SAME, C_REP, C_TRI, C_ONES = (P * i for i in range(6))
C_SLOTMASK = 6 * P
C_BMASK = C_SLOTMASK + GH
C_DMASK = C_BMASK + BPT
C_VALID = C_DMASK + PADN
C_DOWN = C_VALID + 1
C_TILE = C_DOWN + E
C_PADROW = C_TILE + SLOT_TILES
C_HMASK = C_PADROW + 2 * TILES
C_ALL = C_HMASK + GD


def constants():
    p = np.arange(P)
    c = np.zeros((P, C_ALL), np.float32)
    same = p[:, None] // PADN == p[None, :] // PADN
    valid = p % PADN < NP
    c[:, C_IDENT:C_IDENT + P] = np.eye(P)
    c[:, C_MEAN:C_MEAN + P] = (same & valid[:, None]) / np.float32(NP)
    c[:, C_SAME:C_SAME + P] = same
    c[:, C_REP:C_REP + P] = p[:, None] % PADN == p[None, :] % PADN
    c[:, C_TRI:C_TRI + P] = p[:, None] < p[None, :]
    c[:, C_ONES:C_ONES + P] = 1
    c[:, C_SLOTMASK:C_SLOTMASK + GH] = p[:, None] % GD // HD == np.arange(GH)
    c[:, C_BMASK:C_BMASK + BPT] = p[:, None] // PADN == np.arange(BPT)
    c[:, C_DMASK:C_DMASK + PADN] = p[:, None] % PADN == np.arange(PADN)
    c[:, C_VALID] = valid
    c[:, C_DOWN:C_DOWN + E] = E - np.arange(E)
    c[:, C_TILE:C_TILE + SLOT_TILES] = np.arange(SLOT_TILES)
    c[:, C_HMASK:C_HMASK + GD] = p[:, None] // PADN == np.arange(GD) // HD
    spare = SLOTS + np.arange(2 * TILES)[None, :] * P + p[:, None]
    c[:, C_PADROW:C_PADROW + 2 * TILES] = spare * ~valid[:, None]
    return c


class Chain:

    def __init__(self, eng, sem):
        self.eng, self.sem, self.base, self.n = eng, sem, 0, 0

    def add(self, ins):
        ins.then_inc(self.sem, 1)
        self.n += 1

    def wait(self):
        self.eng.wait_ge(self.sem, self.base + self.n)

    def __call__(self, ins):
        self.add(ins)
        self.wait()

    @contextmanager
    def loop(self, start, end, steps):
        before = self.base + self.n
        with self.eng.Fori(start, end) as i:
            self.base, self.n = before + (i - start) * steps, 0
            yield i
            assert self.n == steps, (self.n, steps)
        self.base, self.n = before + (end - start) * steps, 0


def build(nc, xp, wt, rows, attn_w, gate_w, gate_b, w1, b1, w2, b2, const_in, out):
    f32, bf16, i32, u32 = mybir.dt.float32, mybir.dt.bfloat16, mybir.dt.int32, mybir.dt.uint32
    ALU, ACT, AX = mybir.AluOpType, mybir.ActivationFunctionType, mybir.AxisListType

    xs = nc.dram_tensor("slot_rows", (SPARE, D), f32).ap()
    ys = nc.dram_tensor("slot_out", (SLOTS, D), f32).ap()

    ctx = ExitStack()
    with ctx:
        def sb(name, shape, dt=f32):
            return ctx.enter_context(nc.sbuf_tensor(name, shape, dt))

        def sem(name):
            return ctx.enter_context(nc.semaphore(name))

        W1 = sb("W1", [P, E, KC, FF])
        W2 = sb("W2", [P, E, HC, D])
        H = sb("H", [P, TILES, D])
        X = sb("X", [P, TILES, D])
        CO = sb("CO", [P, C_ALL])
        IDB = sb("IDB", [P, P], bf16)
        W2flat = W2[:, :, :, :].rearrange("p e h d -> p (e h d)")
        at = [0]

        def carve(shape, dt=f32):
            n = int(np.prod(shape))
            words = n if dt == f32 else n // 2
            ap = W2flat[:, at[0]:at[0] + words]
            at[0] += words
            if dt != f32:
                ap = ap.bitcast(dt)
            names = "abcde"[:len(shape)]
            kw = dict(zip(names, shape))
            return ap if len(shape) == 1 else ap.rearrange(f"p ({' '.join(names)}) -> p {' '.join(names)}", **kw)

        WT = carve([5, D])
        XP = [carve([5, P]) for _ in range(2)]
        ROWS = carve([3, D])
        AW = carve([4, KC * D])
        TQK = carve([KC, 2, G, 2, GD], bf16)
        TV = carve([KC, D], bf16)
        QS = carve([G, P], bf16)
        KH = carve([G, P], bf16)
        KL = carve([G, P], bf16)
        KXH = carve([G, GH, P], bf16)
        KXL = carve([G, GH, P], bf16)
        S = carve([G * GH, PADN])
        PR = carve([G * GH, PADN])
        PT = carve([G, P])
        VX = carve([BPT, G, GD])
        SIG = carve([TILES, PADN])
        DV = carve([TILES, BPT])
        SREP = carve([TILES * BPT])
        MX = carve([G * GH])
        RS = carve([G * GH])
        XQR = carve([KC, BPT, GH, PADN], bf16)
        assert at[0] <= E * HC * D
        QI = sb("QI", [P, TILES, D], bf16)
        TO = sb("TO", [P, KC, D], bf16)
        XQT = sb("XQT", [P, KC, P], bf16)
        XF = sb("XF", [P, D])
        XT = sb("XT", [P, KC, P])
        ST = sb("ST", [P, TILES, 6])
        MV = sb("MV", [P, 2, TILES])
        SM = sb("SM", [P, 10, TILES])
        AL = sb("AL", [P, 4, 4])
        GW = sb("GW", [P, KC, E])
        GB = sb("GB", [P, E])
        B1 = sb("B1", [P, E * HC])
        B2 = sb("B2", [P, E, D])
        R = sb("R", [P, 10, TILES, E])
        GATE = sb("GATE", [P, 2, TILES])
        SLOT = sb("SLOT", [P, 2, TILES])
        IDX = sb("IDX", [P, 4, TILES], u32)
        ET = sb("ET", [P, SLOT_TILES, E])
        EF = sb("EF", [P, SLOT_TILES])
        EI = sb("EI", [P, SLOT_TILES], i32)
        XG = sb("XG", [P, 2, D])
        XGT = sb("XGT", [P, 2, KC, P])
        HP = QI[:, :, :].rearrange("p t d -> p (t d)").bitcast(f32).rearrange("p (u h) -> p u h", u=2)
        HT = sb("HT", [P, HC, P])
        Y = sb("Y", [P, 2, D])
        ZERO = Y[:, 0, :]

        PS = [ctx.enter_context(nc.psum_tensor(f"PS{i}", [P, 512], f32)) for i in range(8)]
        psT = PS[0][:, 0:KC * P].rearrange("p (k n) -> p k n", k=KC)
        psQ, psK = (PS[i][:, :].rearrange("p (g n) -> p g n", g=G) for i in (1, 2))
        psV = [PS[3 + j // 2][:, (j % 2) * D:(j % 2 + 1) * D] for j in range(BPT)]
        psS = PS[5]
        psPT = PS[6][:, :].rearrange("p (g n) -> p g n", g=G)
        psO = PS[7][:, 0:D]
        psE = [PS[1][:, 0:D], PS[2][:, 0:D]]

        s_const_in = sem("const_in")
        s_embed_w_in = sem("embed_w_in")
        s_attn_w_in = sem("attn_w_in")
        s_misc_in = sem("misc_in")
        s_w1_in = sem("w1_in")
        s_w2_in = sem("w2_in")
        s_zeros_made = sem("zeros_made")
        s_zeros_out = sem("zeros_out")
        s_out_done = sem("out_done")
        s_idb = sem("idb")
        s_abs_sums = sem("abs_sums")
        s_abs_total = sem("abs_total")
        s_embedded = sem("embedded")
        s_biased = sem("biased")
        s_sqrt_in = sem("sqrt_in")
        s_sqrt_out = sem("sqrt_out")
        s_part_sums = sem("part_sums")
        s_batch_means = sem("batch_means")
        s_scale_diag = sem("scale_diag")
        s_scale_rep = sem("scale_rep")
        s_scales_read = sem("scales_read")
        s_quantised = sem("quantised")
        s_q_turned = sem("q_turned")
        s_qT = sem("qT")
        s_q_made = sem("q_made")
        s_k_made = sem("k_made")
        s_v_made = sem("v_made")
        s_q_hi = sem("q_hi")
        s_k_hi = sem("k_hi")
        s_q_split = sem("q_split")
        s_k_low = sem("k_low")
        s_k_spread = sem("k_spread")
        s_v_spread = sem("v_spread")
        s_scored = sem("scored")
        s_s_scaled = sem("s_scaled")
        s_s_centred = sem("s_centred")
        s_probs = sem("probs")
        s_p_turned = sem("p_turned")
        s_pT = sem("pT")
        s_mixed = sem("mixed")
        s_attended = sem("attended")
        s_o_made = sem("o_made")
        s_h_new = sem("h_new")
        s_x2_made = sem("x2_made")
        s_x2_fixed = sem("x2_fixed")
        s_x2_turned = sem("x2_turned")
        s_x2T = sem("x2T")
        s_logits_made = sem("logits_made")
        s_logits_in = sem("logits_in")
        s_logits_centred = sem("logits_centred")
        s_logits_exp = sem("logits_exp")
        s_picks = sem("picks")
        s_ranked = sem("ranked")
        s_routed = sem("routed")
        s_scattered = sem("scattered")
        s_experts_known = sem("experts_known")
        s_xg_turned = sem("xg_turned")
        s_xgT = sem("xgT")
        s_hidden = sem("hidden")
        s_hp_ready = sem("hp_ready")
        s_h_turned = sem("h_turned")
        s_hT = sem("hT")
        s_y_made = sem("y_made")
        s_y_ready = sem("y_ready")
        s_gathered_used = sem("gathered_used")
        s_combined = sem("combined")
        s_dve_step = sem("dve_step")
        s_act_step = sem("act_step")
        s_xp_in = [sem(f"xp_in{u}") for u in range(2)]
        s_xg_in = [sem(f"xg_in{u}") for u in range(2)]
        s_y_out = [sem(f"y_out{u}") for u in range(2)]
        s_gathered = [sem(f"gathered{u}") for u in range(2)]

        def free(eng, semaphore, n):
            if not (isinstance(n, int) and n <= 0):
                eng.wait_ge(semaphore, n)

        def const(a, n):
            return CO[:, a:a + n]

        block = ctx.enter_context(nc.Block())

        @block.sync
        def _(eng):
            eng.dma_start(CO[:, :], const_in).then_inc(s_const_in, 16)
            eng.dma_start(WT, wt).then_inc(s_embed_w_in, 16)
            eng.dma_start(ROWS, rows).then_inc(s_embed_w_in, 16)
            for u in range(2):
                eng.dma_start(XP[u], xp[u]).then_inc(s_xp_in[u], 16)
            with eng.Fori(0, TILES // 2 - 1) as i:
                for u in range(2):
                    eng.wait_ge(s_embedded, 2 * i + u + 1)
                    eng.dma_start(XP[u], xp[bass.ds(2 * i + u + 2, 1)].rearrange("o p c n -> (o p) c n")).then_inc(s_xp_in[u], 16)
            eng.wait_ge(s_attended, TILES)
            for e in range(E):
                eng.dma_start(W2[:, e, :, :], w2[e].rearrange("(h p) d -> p h d", p=P)).then_inc(s_w2_in, 16)

            def load_slots(t, u):
                eng.dma_start(XG[:, u, :], xs[bass.ds(t * P, P), :]).then_inc(s_xg_in[u], 16)

            def store_slots(t, u):
                eng.wait_ge(s_y_ready, t + 1)
                eng.dma_start(ys[bass.ds(t * P, P), :], Y[:, u, :]).then_inc(s_y_out[u], 16)

            eng.wait_ge(s_scattered, 2 * TILES * 16)
            load_slots(0, 0)
            load_slots(1, 1)
            with eng.Fori(0, (SLOT_TILES - 3) // 2) as i:
                for u in range(2):
                    eng.wait_ge(s_xg_turned, 2 * i + u + 1)
                    load_slots(2 * i + u + 2, u)
                    store_slots(2 * i + u, u)
            for t in range(SLOT_TILES - 3, SLOT_TILES):
                if t + 2 < SLOT_TILES:
                    eng.wait_ge(s_xg_turned, t + 1)
                    load_slots(t + 2, t % 2)
                store_slots(t, t % 2)
            o4 = out.rearrange("(t j) n d -> j n t d", j=BPT)
            for q in range(4):
                eng.wait_ge(s_combined, 4 * (q + 1))
                for j in range(BPT):
                    eng.dma_start(o4[j][:, 4 * q:4 * q + 4, :],
                                  H[PADN * j:PADN * j + NP, 4 * q:4 * q + 4, :]).then_inc(s_out_done, 16)
            eng.wait_ge(s_out_done, 16 * 16)

        @block.tensor
        def _(pe):
            mm = nc.tensor.matmul
            pe.wait_ge(s_const_in, 16)
            pe.wait_ge(s_abs_sums, 1)
            mm(PS[0][:, 0:4], const(C_ONES, P), AL[:, 0, :], start=True, stop=True).then_inc(s_abs_total, 1)

            pe.wait_ge(s_embed_w_in, 32)
            def embed(i, u, free):
                pe.wait_ge(s_xp_in[u], 16 * (i + 1))
                if free is not None:
                    pe.wait_ge(s_biased, free)
                for k in range(5):
                    last = mm(psE[u], XP[u][:, k, :], WT[:, k, :], start=k == 0, stop=k == 4)
                last.then_inc(s_embedded, 1)

            for u in range(2):
                embed(0, u, None)
            with pe.Fori(1, TILES // 2) as i:
                for u in range(2):
                    embed(i, u, 2 * i + u - 1)

            def batch_means(n):
                for m in range(2):
                    pe.wait_ge(s_part_sums, 2 * n + m + 1)
                    mm(PS[0][:, 0:TILES], const(C_MEAN, P), SM[:, m, :], start=True, stop=True).then_inc(s_batch_means, 1)

            batch_means(0)
            pe.wait_ge(s_scale_diag, 2)
            mm(PS[1][:, 0:TILES * BPT], const(C_REP, P), DV.rearrange("p t b -> p (t b)"), start=True, stop=True).then_inc(s_scale_rep, 1)
            mm(PS[2][:, :], const(C_SAME, P), SIG.rearrange("p t n -> p (t n)"), start=True, stop=True).then_inc(s_scale_rep, 1)

            def turn(t):
                for k in range(KC):
                    last = mm(psT[:, k, :], QI[:, t, k * P:(k + 1) * P], IDB[:, :], start=True, stop=True)
                return last

            def project(t):
                free(pe, s_qT, t)
                turn(t).then_inc(s_q_turned, 1)
                pe.wait_ge(s_qT, t + 1)
                free(pe, s_q_split, t)
                for m, ps, done in ((0, psQ, s_q_made), (1, psK, s_k_made)):
                    if m:
                        free(pe, s_k_low, t)
                    for g in range(G):
                        for k in range(KC):
                            last = mm(ps[:, g, :], TQK[:, k, m, g, :, :], XQR[:, k, :, 0, :], start=k == 0, stop=k == KC - 1)
                    last.then_inc(done, 1)
                free(pe, s_v_spread, t)
                for j in range(BPT):
                    for k in range(KC):
                        keys = XQR[:, k, j, :, :].rearrange("p r n -> p (r n)")
                        last = mm(psV[j], keys, TV[:, k, :], start=k == 0, stop=k == KC - 1)
                last.then_inc(s_v_made, 1)
                pe.wait_ge(s_q_split, t + 1)
                pe.wait_ge(s_k_spread, t + 1)
                free(pe, s_s_scaled, t)
                for j in range(BPT):
                    r = slice(j * PADN, (j + 1) * PADN)
                    for g in range(G):
                        for part, kx in enumerate((KXH, KXL)):
                            last = mm(psS[r, g * P:(g + 1) * P], QS[:, g, r], kx[:, g, :, r], start=part == 0, stop=part == 1)
                last.then_inc(s_scored, 1)

            def mix(t):
                pe.wait_ge(s_probs, t + 1)
                free(pe, s_pT, t)
                for g in range(G):
                    last = nc.tensor.transpose(psPT[:, g, :], PR[:, g * GH:(g + 1) * GH, :].rearrange("p h n -> p (h n)"), const(C_IDENT, P))
                last.then_inc(s_p_turned, 1)
                pe.wait_ge(s_pT, t + 1)
                pe.wait_ge(s_v_spread, t + 1)
                free(pe, s_attended, t)
                for j in range(BPT):
                    r = slice(j * PADN, (j + 1) * PADN)
                    for g in range(G):
                        last = mm(psO[r, g * GD:(g + 1) * GD], PT[:, g, r], VX[:, j, g, :], start=True, stop=True)
                last.then_inc(s_mixed, 1)

            pe.wait_ge(s_quantised, 1)
            pe.wait_ge(s_scales_read, 1)
            pe.wait_ge(s_idb, 1)
            project(0)
            project(1)
            mix(0)
            with pe.Fori(2, TILES) as t:
                project(t)
                mix(t - 1)
            mix(TILES - 1)

            batch_means(1)
            pe.wait_ge(s_quantised, 2)

            def project_out(t):
                pe.wait_ge(s_qT, t + TILES)
                turn(t).then_inc(s_q_turned, 1)
                pe.wait_ge(s_qT, t + TILES + 1)
                free(pe, s_h_new, t)
                for k in range(KC):
                    last = mm(psO, XQT[:, k, :], TO[:, k, :], start=k == 0, stop=k == KC - 1)
                last.then_inc(s_o_made, 1)

            project_out(0)
            with pe.Fori(1, TILES) as t:
                project_out(t)

            pe.wait_ge(s_misc_in, 64)

            def logits(t):
                pe.wait_ge(s_x2_fixed, t + 1)
                free(pe, s_x2T, t)
                for k in range(KC):
                    last = nc.tensor.transpose(psT[:, k, :], XF[:, k * P:(k + 1) * P], const(C_IDENT, P))
                last.then_inc(s_x2_turned, 1)
                pe.wait_ge(s_x2T, t + 1)
                free(pe, s_logits_in, t)
                for k in range(KC):
                    last = mm(PS[1][:, 0:E], XT[:, k, :], GW[:, k, :], start=k == 0, stop=k == KC - 1)
                last.then_inc(s_logits_made, 1)

            logits(0)
            with pe.Fori(1, TILES) as t:
                logits(t)
            pe.wait_ge(s_picks, 1)
            oh = R[:, 0, :, :].rearrange("p t e -> p (t e)")
            mm(PS[1][:, 0:TILES * E], const(C_TRI, P), oh, start=True, stop=True).then_inc(s_ranked, 1)
            mm(PS[2][:, 0:TILES * E], const(C_ONES, P), oh, start=True, stop=True).then_inc(s_ranked, 1)

            def expert(t):
                return pe.value_load(EI[0:1, bass.ds(t, 1)], min_val=0, max_val=E - 1)

            def turn_x(t, u, i):
                pe.wait_ge(s_xg_in[u], 16 * (i + 1))
                free(pe, s_xgT, t)
                for k in range(KC):
                    last = nc.tensor.transpose(psT[:, k, :], XG[:, u, k * P:(k + 1) * P], const(C_IDENT, P))
                last.then_inc(s_xg_turned, 1)

            def hidden(t, u):
                pe.wait_ge(s_xgT, t + 1)
                e = expert(t)
                free(pe, s_hp_ready, t - 1)
                for half in range(2):
                    for k in range(KC):
                        last = mm(PS[1 + 2 * u + half][:, :], XGT[:, u, k, :], W1[:, e, k, half * 512:(half + 1) * 512],
                                  start=k == 0, stop=k == KC - 1)
                last.then_inc(s_hidden, 1)

            def turn_h(t, u):
                pe.wait_ge(s_hp_ready, t + 1)
                free(pe, s_hT, t)
                for h in range(HC):
                    last = nc.tensor.transpose(PS[5 + h // 4][:, (h % 4) * P:(h % 4 + 1) * P],
                                               HP[:, u, h * P:(h + 1) * P], const(C_IDENT, P))
                last.then_inc(s_h_turned, 1)

            def output(t):
                e = expert(t)
                pe.wait_ge(s_hT, t + 1)
                free(pe, s_y_ready, t)
                for h in range(HC):
                    last = mm(PS[7][:, 0:D], HT[:, h, :], W2[:, e, h, :], start=h == 0, stop=h == HC - 1)
                last.then_inc(s_y_made, 1)

            pe.wait_ge(s_experts_known, 1)
            pe.wait_ge(s_w1_in, 16 * E)
            turn_x(0, 0, 0)
            hidden(0, 0)
            turn_x(1, 1, 0)
            pe.wait_ge(s_w2_in, 16 * E)

            def experts(i):
                for u in range(2):
                    t = 2 * i + u
                    turn_h(t, u)
                    hidden(t + 1, 1 - u)
                    turn_x(t + 2, u, i + 1)
                    output(t)

            experts(0)
            with pe.Fori(1, (SLOT_TILES - 3) // 2) as i:
                experts(i)
            for t in range(SLOT_TILES - 3, SLOT_TILES):
                turn_h(t, t % 2)
                if t + 1 < SLOT_TILES:
                    hidden(t + 1, (t + 1) % 2)
                if t + 2 < SLOT_TILES:
                    turn_x(t + 2, t % 2, t // 2 + 1)
                output(t)

        @block.scalar
        def _(act):
            act.dma_start(AW, attn_w).then_inc(s_attn_w_in, 16)
            act.dma_start(GW[:, :, :], gate_w).then_inc(s_misc_in, 16)
            act.dma_start(GB[:, :], gate_b).then_inc(s_misc_in, 16)
            act.dma_start(B1[:, :], b1).then_inc(s_misc_in, 16)
            act.dma_start(B2[:, :, :], b2).then_inc(s_misc_in, 16)
            for e in range(E):
                act.dma_start(W1[:, e, :, :], w1[e].rearrange("(k p) h -> p k h", p=P)).then_inc(s_w1_in, 16)

            def roots(n, count):
                for m in range(count):
                    act.wait_ge(s_sqrt_in, n + m + 1)
                    nc.scalar.activation(SM[:, 3, :], SM[:, 2, :], ACT.Sqrt).then_inc(s_sqrt_out, 1)

            roots(0, 3)

            def take_turned(t, n):
                act.wait_ge(s_q_turned, n + 1)
                nc.scalar.activation(XQT[:, :, :], psT, ACT.Copy).then_inc(s_qT, 1)

            def split(t):
                free(act, s_v_made, t)
                act.wait_ge(s_q_turned, t + 1)
                for k in range(KC):
                    last = nc.scalar.activation(
                        XQR[:, k], psT[:, k, :].rearrange("p (b n) -> p b n", b=BPT).unsqueeze(2).to_broadcast([P, BPT, GH, PADN]),
                        ACT.Copy)
                last.then_inc(s_qT, 1)
                act.wait_ge(s_q_made, t + 1)
                free(act, s_scored, t)
                nc.scalar.activation(QS, psQ, ACT.Copy).then_inc(s_q_hi, 1)
                act.wait_ge(s_k_made, t + 1)
                free(act, s_k_spread, t)
                nc.scalar.activation(KH, psK, ACT.Copy).then_inc(s_k_hi, 1)

            def take_probs(t):
                act.wait_ge(s_p_turned, t + 1)
                free(act, s_mixed, t)
                nc.scalar.activation(PT, psPT, ACT.Copy).then_inc(s_pT, 1)

            def exps(t):
                act.wait_ge(s_s_centred, t + 2)
                free(act, s_p_turned, t)
                nc.scalar.activation(PR[:, :, 0:NP], S[:, :, 0:NP], ACT.Exp).then_inc(s_probs, 1)

            split(0)
            exps(0)
            split(1)
            take_probs(0)
            exps(1)
            with act.Fori(2, TILES) as t:
                split(t)
                take_probs(t - 1)
                exps(t)
            take_probs(TILES - 1)
            roots(3, 1)

            def turned_out(t):
                free(act, s_o_made, t)
                take_turned(t, t + TILES)

            turned_out(0)
            with act.Fori(1, TILES) as t:
                turned_out(t)
            roots(4, 1)

            def tokens_turned(t):
                act.wait_ge(s_x2_made, t + 1)
                free(act, s_x2_turned, t)
                nc.scalar.activation(XF[:, :], X[:, t, :], ACT.Copy).then_inc(s_x2_fixed, 1)
                act.wait_ge(s_x2_turned, t + 1)
                free(act, s_logits_made, t)
                nc.scalar.activation(XT[:, :, :], psT, ACT.Copy).then_inc(s_x2T, 1)

            tokens_turned(0)
            with act.Fori(1, TILES) as t:
                tokens_turned(t)
            act.wait_ge(s_logits_centred, 1)
            nc.scalar.activation(R[:, 1, :, :], R[:, 2, :, :], ACT.Exp).then_inc(s_logits_exp, 1)

            def take_x(t, u):
                act.wait_ge(s_xg_turned, t + 1)
                free(act, s_hidden, t - 1)
                nc.scalar.activation(XGT[:, u, :, :], psT, ACT.Copy).then_inc(s_xgT, 1)

            def relu(t):
                e = act.value_load(EI[0:1, bass.ds(t, 1)], min_val=0, max_val=E - 1)
                act.wait_ge(s_h_turned, t + 1)
                free(act, s_y_made, t)
                for h in range(HC):
                    last = nc.scalar.activation(HT[:, h, :], PS[5 + h // 4][:, (h % 4) * P:(h % 4 + 1) * P], ACT.Relu,
                                                bias=B1[:, bass.ds(e * HC + h, 1)])
                last.then_inc(s_hT, 1)

            act.wait_ge(s_experts_known, 1)
            take_x(0, 0)
            take_x(1, 1)

            def experts(i):
                for u in range(2):
                    relu(2 * i + u)
                    take_x(2 * i + u + 2, u)

            experts(0)
            with act.Fori(1, (SLOT_TILES - 3) // 2) as i:
                experts(i)
            for t in range(SLOT_TILES - 3, SLOT_TILES):
                relu(t)
                if t + 2 < SLOT_TILES:
                    take_x(t + 2, t % 2)

        @block.gpsimd
        def _(pool):
            pool.wait_ge(s_zeros_made, 1)
            for c in range(SLOT_TILES):
                pool.dma_start(xs[c * P:(c + 1) * P, :], ZERO).then_inc(s_zeros_out, 16)
            pool.wait_ge(s_zeros_out, 16 * SLOT_TILES)
            pool.wait_ge(s_routed, 1)
            for t in range(TILES):
                for k in range(2):
                    pool.indirect_dma_start(xs, bass.IndirectOffsetOnAxis(ap=IDX[:, k, t:t + 1], axis=0),
                                            X[:, t, :], None).then_inc(s_scattered, 16)
            for u in range(2):
                pool.wait_ge(s_y_out[u], 16 * ((SLOT_TILES + 1 - u) // 2))
            for t in range(TILES):
                if t >= 2:
                    free(pool, s_combined, t - 1)
                for k in range(2):
                    pool.indirect_dma_start(HP[:, t % 2, k * D:(k + 1) * D], None, ys,
                                            bass.IndirectOffsetOnAxis(ap=IDX[:, 2 + k, t:t + 1], axis=0)).then_inc(s_gathered[t % 2], 16)

        @block.vector
        def _(dve):
            v = nc.vector
            step = Chain(dve, s_dve_step)
            MEAN, VAR = MV[:, 0, :], MV[:, 1, :]

            def col(i):
                return SM[:, i, :]

            def root_inverse(n):
                dve.wait_ge(s_sqrt_out, n + 1)
                step(v.reciprocal(col(4), col(3)))
                step(v.tensor_tensor(col(5), col(4), col(4), ALU.mult))
                step(v.tensor_tensor(col(5), col(5), col(2), ALU.mult))
                step(v.tensor_scalar(col(5), col(5), -0.5, 1.5, ALU.mult, ALU.add))
                step(v.tensor_tensor(col(4), col(4), col(5), ALU.mult))

            def row_stats(src):
                with step.loop(0, TILES, 1) as t:
                    step.add(v.bn_stats(ST[:, t, :], src[:, t, :]))
                step.wait()
                step.add(v.tensor_tensor(MEAN, ST[:, :, 1], ST[:, :, 4], ALU.add))
                step.add(v.tensor_tensor(col(5), ST[:, :, 1], ST[:, :, 4], ALU.subtract))
                step(v.tensor_tensor(VAR, ST[:, :, 2], ST[:, :, 5], ALU.add))
                step.add(v.tensor_scalar(MEAN, MEAN, 0.5, None, ALU.mult))
                step(v.scalar_tensor_tensor(col(5), col(5), 0.25, col(5), ALU.mult, ALU.mult))
                step(v.scalar_tensor_tensor(VAR, VAR, 1.0 / D, col(5), ALU.mult, ALU.add))

            def row_norms(src, n):
                row_stats(src)
                v.tensor_scalar(col(2), VAR, EPS, None, ALU.add).then_inc(s_sqrt_in, 1)
                dve.wait_ge(s_sqrt_in, n + 1)
                root_inverse(n)

            def quantise(n):
                row_stats(X)
                v.tensor_copy(col(0), MEAN).then_inc(s_part_sums, 1)
                dve.wait_ge(s_batch_means, 2 * n + 1)
                step(v.tensor_copy(col(7), PS[0][:, 0:TILES]))
                step(v.tensor_tensor(col(5), MEAN, col(7), ALU.subtract))
                step(v.tensor_tensor(col(5), col(5), col(5), ALU.mult))
                v.tensor_tensor(col(1), col(5), VAR, ALU.add).then_inc(s_part_sums, 1)
                dve.wait_ge(s_batch_means, 2 * n + 2)
                r = 2 if n == 0 else 3
                v.tensor_scalar(col(2), PS[0][:, 0:TILES], EPS, None, ALU.add).then_inc(s_sqrt_in, 1)
                dve.wait_ge(s_sqrt_in, r + 1)
                root_inverse(r)
                with step.loop(0, TILES, 1) as t:
                    step.add(v.tensor_scalar(X[:, t, :], X[:, t, :], SM[:, 7, bass.ds(t, 1)], SM[:, 4, bass.ds(t, 1)],
                                             ALU.subtract, ALU.mult))
                step.wait()
                step(v.tensor_reduce(col(5), X[:, :, :], AX.X, ALU.max, apply_absolute_value=True))
                step(v.tensor_scalar(col(5), col(5), 1e-5, None, ALU.max))
                step.add(v.tensor_scalar(col(6), col(5), 1.0 / 127.0, None, ALU.mult))
                step(v.reciprocal(col(8), col(5)))
                step(v.tensor_scalar(col(8), col(8), 127.0, None, ALU.mult))
                with step.loop(0, TILES, 1) as t:
                    step.add(v.tensor_scalar(X[:, t, :], X[:, t, :], SM[:, 8, bass.ds(t, 1)], MAGIC, ALU.mult, ALU.add))
                step.wait()
                step(v.tensor_scalar(X[:, :, :], X[:, :, :], MAGIC - 128.0, MAGIC + 127.0, ALU.max, ALU.min))
                v.tensor_scalar(QI[:, :, :], X[:, :, :], -MAGIC, None, ALU.add).then_inc(s_quantised, 1)
                dve.wait_ge(s_quantised, n + 1)

            v.memset(ZERO, 0.0).then_inc(s_zeros_made, 1)
            dve.wait_ge(s_const_in, 16)
            v.tensor_copy(IDB[:, :], const(C_IDENT, P)).then_inc(s_idb, 1)
            dve.wait_ge(s_attn_w_in, 16)
            v.tensor_reduce(AL[:, 0, :], AW, AX.X, ALU.add, apply_absolute_value=True).then_inc(s_abs_sums, 1)
            dve.wait_ge(s_abs_total, 1)
            step(v.tensor_scalar(AL[:, 1, :], PS[0][:, 0:4], 1.0 / (D * D), 1e-5, ALU.mult, ALU.max))
            step(v.reciprocal(AL[:, 2, :], AL[:, 1, :]))
            for m in range(4):
                step.add(v.tensor_scalar(AW[:, m, :], AW[:, m, :], AL[:, 2, m:m + 1], MAGIC, ALU.mult, ALU.add))
            step.wait()
            step(v.tensor_scalar(AW, AW, -MAGIC, 1.0, ALU.add, ALU.min))
            awv = AW.rearrange("p m (k g c) -> p m k g c", k=KC, g=G)
            for m in range(2):
                for r in range(2):
                    for k in range(KC):
                        step.add(v.tensor_scalar(TQK[:, k, m, :, r, :], awv[:, m, k, :, :], -1.0, None, ALU.max))
            for m, dst in ((2, TV), (3, TO[:, :, :])):
                step.add(v.tensor_scalar(dst, AW[:, m, :].rearrange("p (k c) -> p k c", k=KC), -1.0, None, ALU.max))
            step(v.tensor_scalar(AL[:, 3, 0:1], AL[:, 1, 0:1], AL[:, 1, 1:2], HD ** -0.5, ALU.mult, ALU.mult))
            v.memset(PR, 0.0).then_inc(s_s_centred, 1)

            dve.wait_ge(s_embed_w_in, 32)
            with dve.Fori(0, TILES // 2) as i:
                for u in range(2):
                    dve.wait_ge(s_embedded, 2 * i + u + 1)
                    v.tensor_tensor(X[:, 2 * i + u, :], psE[u], ROWS[:, 0, :], ALU.add).then_inc(s_biased, 1)
            dve.wait_ge(s_biased, TILES)
            row_norms(X, 0)
            with step.loop(0, TILES, 1) as t:
                step.add(v.tensor_scalar(X[:, t, :], X[:, t, :], MV[:, 0, bass.ds(t, 1)], SM[:, 4, bass.ds(t, 1)], ALU.subtract, ALU.mult))
            step.wait()
            step(v.tensor_tensor(X[:, :, :], X[:, :, :], ROWS[:, 1:2, :].to_broadcast([P, TILES, D]), ALU.mult))
            step(v.tensor_tensor(H[:, :, :], X[:, :, :], ROWS[:, 2:3, :].to_broadcast([P, TILES, D]), ALU.add))
            row_norms(H, 1)
            with step.loop(0, TILES, 1) as t:
                step.add(v.tensor_scalar(X[:, t, :], H[:, t, :], MV[:, 0, bass.ds(t, 1)], SM[:, 4, bass.ds(t, 1)], ALU.subtract, ALU.mult))
            step.wait()
            quantise(0)

            scale = SM[:, 6, :].unsqueeze(2)
            v.tensor_tensor(DV, scale.to_broadcast([P, TILES, BPT]),
                            const(C_BMASK, BPT).unsqueeze(1).to_broadcast([P, TILES, BPT]), ALU.mult).then_inc(s_scale_diag, 1)
            v.tensor_tensor(SIG, scale.to_broadcast([P, TILES, PADN]),
                            const(C_DMASK, PADN).unsqueeze(1).to_broadcast([P, TILES, PADN]), ALU.mult).then_inc(s_scale_diag, 1)
            dve.wait_ge(s_scale_rep, 2)
            step(v.tensor_scalar(SREP, PS[1][:, 0:TILES * BPT], AL[:, 1, 2:3], None, ALU.mult))
            v.scalar_tensor_tensor(SIG, PS[2][:, :].rearrange("p (t n) -> p t n", t=TILES), AL[:, 3, 0:1],
                                   scale.to_broadcast([P, TILES, PADN]), ALU.mult, ALU.mult).then_inc(s_scales_read, 1)
            dve.wait_ge(s_scales_read, 1)

            def split(t):
                dve.wait_ge(s_q_hi, t + 1)
                v.tensor_tensor(QS[GD:P], psQ[GD:P], QS[GD:P], ALU.subtract).then_inc(s_q_split, 1)
                dve.wait_ge(s_k_hi, t + 1)
                free(dve, s_k_spread, t)
                v.tensor_tensor(KL, psK, KH, ALU.subtract).then_inc(s_k_low, 1)
                dve.wait_ge(s_k_low, t + 1)
                free(dve, s_scored, t)
                for h in range(GH):
                    for src, dst in ((KH, KXH), (KL, KXL)):
                        last = v.tensor_scalar(dst[:, :, h, :], src, CO[:, C_SLOTMASK + h:C_SLOTMASK + h + 1], None, ALU.mult)
                last.then_inc(s_k_spread, 1)

            def softmax(t):
                dve.wait_ge(s_scored, t + 1)
                free(dve, s_probs, t)
                v.tensor_tensor(S, psS[:, :].rearrange("p (h n) -> p h n", n=PADN),
                                SIG[:, bass.ds(t, 1), :].to_broadcast([P, G * GH, PADN]), ALU.mult).then_inc(s_s_scaled, 1)
                dve.wait_ge(s_s_scaled, t + 1)
                step(v.tensor_reduce(MX, S[:, :, 0:NP], AX.X, ALU.max))
                v.tensor_tensor(S[:, :, 0:NP], S[:, :, 0:NP], MX.unsqueeze(2).to_broadcast([P, G * GH, NP]),
                                ALU.subtract).then_inc(s_s_centred, 1)

            def attend(t):
                dve.wait_ge(s_mixed, t + 1)
                v.tensor_tensor(X[:, t, :].rearrange("p (h d) -> p h d", d=HD), psO.rearrange("p (h d) -> p h d", d=HD),
                                RS.unsqueeze(2).to_broadcast([P, G * GH, HD]), ALU.mult).then_inc(s_attended, 1)

            def spread_v(t):
                dve.wait_ge(s_v_made, t + 1)
                for j in range(BPT):
                    last = v.scalar_tensor_tensor(
                        VX[:, j], psV[j].rearrange("p (g c) -> p g c", g=G), SREP[:, bass.ds(t * BPT + j, 1)],
                        const(C_HMASK, GD).unsqueeze(1).to_broadcast([P, G, GD]), ALU.mult, ALU.mult)
                last.then_inc(s_v_spread, 1)

            def sums(t):
                dve.wait_ge(s_probs, t + 1)
                free(dve, s_attended, t)
                step(v.tensor_reduce(RS, PR[:, :, 0:NP], AX.X, ALU.add))
                step(v.reciprocal(RS, RS))

            split(0)
            softmax(0)
            spread_v(0)
            sums(0)

            def attention(t):
                split(t)
                softmax(t)
                attend(t - 1)
                spread_v(t)
                sums(t)

            attention(1)
            with step.loop(2, TILES, 3) as t:
                attention(t)
            attend(TILES - 1)
            dve.wait_ge(s_attended, TILES)
            quantise(1)
            step.add(v.tensor_scalar(col(6), col(6), AL[:, 1, 3:4], None, ALU.mult))
            step.wait()
            with dve.Fori(0, TILES) as t:
                dve.wait_ge(s_o_made, t + 1)
                v.scalar_tensor_tensor(H[:, t, :], psO, SM[:, 6, bass.ds(t, 1)], H[:, t, :], ALU.mult, ALU.add).then_inc(s_h_new, 1)
            dve.wait_ge(s_h_new, TILES)
            row_norms(H, 4)
            with dve.Fori(0, TILES) as t:
                v.tensor_scalar(X[:, t, :], H[:, t, :], MV[:, 0, bass.ds(t, 1)], SM[:, 4, bass.ds(t, 1)], ALU.subtract, ALU.mult).then_inc(s_x2_made, 1)
            dve.wait_ge(s_misc_in, 64)
            with dve.Fori(0, TILES) as t:
                dve.wait_ge(s_logits_made, t + 1)
                v.tensor_tensor(R[:, 1, t, :], PS[1][:, 0:E], GB[:, :], ALU.add).then_inc(s_logits_in, 1)
            dve.wait_ge(s_logits_in, TILES)

            def r(i):
                return R[:, i, :, :]

            def wide(i):
                return SM[:, i, :].unsqueeze(2).to_broadcast([P, TILES, E])

            down = const(C_DOWN, E).unsqueeze(1).to_broadcast([P, TILES, E])
            step(v.tensor_reduce(col(0), r(1), AX.X, ALU.max))
            v.tensor_tensor(r(2), r(1), wide(0), ALU.subtract).then_inc(s_logits_centred, 1)
            dve.wait_ge(s_logits_exp, 1)
            step(v.tensor_reduce(col(1), r(1), AX.X, ALU.add))
            step(v.reciprocal(col(1), col(1)))
            for k in range(2):
                step(v.tensor_reduce(col(0), r(1), AX.X, ALU.max))
                step.add(v.tensor_tensor(GATE[:, k, :], col(0), col(1), ALU.mult))
                step(v.tensor_tensor(r(2), r(1), wide(0), ALU.is_ge))
                step(v.tensor_tensor(r(2), r(2), down, ALU.mult))
                step(v.tensor_reduce(col(2), r(2), AX.X, ALU.max))
                step(v.tensor_tensor(r(3 + k), down, wide(2), ALU.is_equal))
                if k == 0:
                    step(v.scalar_tensor_tensor(r(1), r(3), -2.0, r(1), ALU.mult, ALU.add))
            step(v.tensor_tensor(r(0), r(3), r(4), ALU.add))
            v.tensor_scalar(r(0), r(0), CO[:, C_VALID:C_VALID + 1], None, ALU.mult).then_inc(s_picks, 1)
            dve.wait_ge(s_ranked, 2)
            step(v.tensor_copy(r(5), PS[2][:, 0:TILES * E].rearrange("p (t e) -> p t e", e=E)))
            a, b = 5, 6
            for d in (1, 2, 4, 8):
                step.add(v.tensor_copy(R[:, b, 0:d, :], R[:, a, 0:d, :]))
                step(v.tensor_tensor(R[:, b, d:, :], R[:, a, d:, :], R[:, a, 0:TILES - d, :], ALU.add))
                a, b = b, a
            count = R[:, a, TILES - 1, :]
            cum = R[:, 7, 0, :]
            cum2 = R[:, 7, 1, :]
            step(v.tensor_scalar(cum, count, 1.0 / P, (P - 1) / P - (P - 1) / (2 * P), ALU.mult, ALU.add))
            step(v.tensor_scalar(cum, cum, MAGIC, -MAGIC, ALU.add, ALU.add))
            step(v.tensor_copy(R[:, 7, 2, :], cum))
            x, y = 0, 1
            for d in (1, 2, 4):
                step.add(v.tensor_copy(R[:, 7, y, 0:d], R[:, 7, x, 0:d]))
                step(v.tensor_tensor(R[:, 7, y, d:], R[:, 7, x, d:], R[:, 7, x, 0:E - d], ALU.add))
                x, y = y, x
            step(v.tensor_tensor(R[:, 7, 2, :], R[:, 7, x, :], R[:, 7, 2, :], ALU.subtract))
            step(v.tensor_scalar(R[:, 7, 2, :], R[:, 7, 2, :], float(P), None, ALU.mult))
            step(v.tensor_tensor(ET[:, :, :], const(C_TILE, SLOT_TILES).unsqueeze(2).to_broadcast([P, SLOT_TILES, E]),
                                 R[:, 7, x:x + 1, :].to_broadcast([P, SLOT_TILES, E]), ALU.is_ge))
            step(v.tensor_reduce(EF[:, :], ET[:, :, :], AX.X, ALU.add))
            v.tensor_scalar(EI[:, :], EF[:, :], float(E - 1), None, ALU.min).then_inc(s_experts_known, 1)
            step(v.tensor_tensor(r(8), PS[1][:, 0:TILES * E].rearrange("p (t e) -> p t e", e=E),
                                 R[:, 7, 2:3, :].to_broadcast([P, TILES, E]), ALU.add))
            step(v.tensor_tensor(R[:, 8, 1:, :], R[:, 8, 1:, :], R[:, a, 0:TILES - 1, :], ALU.add))
            for k in range(2):
                step(v.tensor_tensor(r(9), r(8), r(3 + k), ALU.mult))
                step(v.tensor_reduce(SLOT[:, k, :], r(9), AX.X, ALU.add))
                step(v.tensor_scalar(SLOT[:, k, :], SLOT[:, k, :], CO[:, C_VALID:C_VALID + 1], None, ALU.mult))
                step.add(v.tensor_copy(IDX[:, 2 + k, :], SLOT[:, k, :]))
                last = v.tensor_tensor(IDX[:, k, :], SLOT[:, k, :], const(C_PADROW + k * TILES, TILES), ALU.add)
                if k:
                    last.then_inc(s_routed, 1)
                else:
                    step.add(last)

            def take_hidden(t, u):
                dve.wait_ge(s_hidden, t + 1)
                free(dve, s_h_turned, t - 1)
                for half in range(2):
                    last = v.tensor_copy(HP[:, u, half * 512:(half + 1) * 512], PS[1 + 2 * u + half][:, :])
                last.then_inc(s_hp_ready, 1)

            def take_y(t, u, i):
                e = dve.value_load(EI[0:1, bass.ds(t, 1)], min_val=0, max_val=E - 1)
                dve.wait_ge(s_y_made, t + 1)
                free(dve, s_y_out[u], 16 * i)
                v.tensor_tensor(Y[:, u, :], PS[7][:, 0:D], B2[:, e, :], ALU.add).then_inc(s_y_ready, 1)

            dve.wait_ge(s_experts_known, 1)
            take_hidden(0, 0)
            dve.wait_ge(s_zeros_out, 16 * SLOT_TILES)

            def experts(i):
                for u in range(2):
                    take_hidden(2 * i + u + 1, 1 - u)
                    take_y(2 * i + u, u, i)

            experts(0)
            with dve.Fori(1, (SLOT_TILES - 3) // 2) as i:
                experts(i)
            for t in range(SLOT_TILES - 3, SLOT_TILES):
                if t + 1 < SLOT_TILES:
                    take_hidden(t + 1, (t + 1) % 2)
                take_y(t, t % 2, t // 2)

            for t in range(TILES):
                dve.wait_ge(s_gathered[t % 2], 32 * (t // 2 + 1))
                step(v.scalar_tensor_tensor(H[:, t, :], HP[:, t % 2, 0:D], GATE[:, 0, t:t + 1], H[:, t, :], ALU.mult, ALU.add))
                v.scalar_tensor_tensor(H[:, t, :], HP[:, t % 2, D:2 * D], GATE[:, 1, t:t + 1], H[:, t, :],
                                       ALU.mult, ALU.add).then_inc(s_combined, 1)


def kernel(x, L0_tok_W, L0_tok_b, L0_tok_gamma, L0_tok_beta, L0_attn_w_q, L0_attn_w_k, L0_attn_w_v, L0_attn_w_o,
           L0_ffn_gate_w, L0_ffn_gate_b, L0_ffn_w1, L0_ffn_b1, L0_ffn_w2, L0_ffn_b2):
    import concourse.bacc as bacc
    from concourse.bass_utils import run_bass_kernel_spmd

    def wide(a):
        return np.broadcast_to(a, (P,) + a.shape)

    x = np.asarray(x)
    pixels = np.zeros((B, MELS, PF, PADN), x.dtype)
    for f in range(PF):
        pixels[:, :, f, :NP] = x[:, :, f:f + HOP * (NP - 1) + 1:HOP]
    xp = pixels.reshape(TILES, BPT, 5, P, PADN).transpose(0, 3, 2, 1, 4).reshape(TILES, P, 5, P)
    wt = np.asarray(L0_tok_W).reshape(5, P, D).transpose(1, 0, 2)
    attn = [np.asarray(a).T.reshape(KC, P, D).transpose(1, 0, 2).reshape(P, KC * D)
            for a in (L0_attn_w_q, L0_attn_w_k, L0_attn_w_v, L0_attn_w_o)]
    arrays = {
        "xp": xp, "wt": wt,
        "rows": wide(np.stack([np.asarray(a) for a in (L0_tok_b, L0_tok_gamma, L0_tok_beta)])),
        "attn_w": np.stack(attn, 1),
        "gate_w": np.asarray(L0_ffn_gate_w).T.reshape(KC, P, E).transpose(1, 0, 2),
        "gate_b": wide(np.asarray(L0_ffn_gate_b)),
        "w1": np.asarray(L0_ffn_w1),
        "b1": np.asarray(L0_ffn_b1).reshape(E * HC, P).T,
        "w2": np.asarray(L0_ffn_w2),
        "b2": wide(np.asarray(L0_ffn_b2)),
        "const": constants(),
    }
    arrays = {f"in_{k}": np.ascontiguousarray(a) for k, a in arrays.items()}
    nc = bacc.Bacc("TRN2", target_bir_lowering=False, num_devices=1)
    args = [nc.dram_tensor(k, a.shape, mybir.dt.from_np(a.dtype), kind="ExternalInput").ap() for k, a in arrays.items()]
    args.append(nc.dram_tensor("out", (B, NP, D), mybir.dt.float32, kind="ExternalOutput").ap())
    build(nc, *args)
    r = run_bass_kernel_spmd(nc, [arrays], core_ids=[0])
    return r.results[0]["out"]
```

```python
from contextlib import ExitStack, contextmanager

import numpy as np
import concourse.bass as bass
from concourse import mybir

B, MELS, FRAMES = 64, 80, 125
PF, HOP, NP = 8, 4, 30
D, NH, HD = 256, 16, 16
E, FF = 8, 1024
P = 128
PADN = 32
BPT = P // PADN
TILES = B // BPT
KC = D // P
HC = FF // P
G, GH = 4, 4
GD = GH * HD
SLOT_TILES = B * NP * 2 // P + E - 1
BEYOND = 4096
EPS = 1e-5
MAGIC = 1.5 * 2.0 ** 23

C_IDENT, C_MEAN, C_SAME, C_REP, C_TRI, C_ONES = (P * i for i in range(6))
C_SLOTMASK = 6 * P
C_BMASK = C_SLOTMASK + GH
C_DMASK = C_BMASK + BPT
C_VALID = C_DMASK + PADN
C_DOWN = C_VALID + 1
C_TILE = C_DOWN + E
C_TOKEN = C_TILE + SLOT_TILES
C_ROW = C_TOKEN + 2 * 2 * TILES
C_HMASK = C_ROW + P
C_ALL = C_HMASK + GD


def constants():
    p = np.arange(P)
    c = np.zeros((P, C_ALL), np.float32)
    same = p[:, None] // PADN == p[None, :] // PADN
    valid = p % PADN < NP
    c[:, C_IDENT:C_IDENT + P] = np.eye(P)
    c[:, C_MEAN:C_MEAN + P] = (same & valid[:, None]) / np.float32(NP)
    c[:, C_SAME:C_SAME + P] = same
    c[:, C_REP:C_REP + P] = p[:, None] % PADN == p[None, :] % PADN
    c[:, C_TRI:C_TRI + P] = p[:, None] < p[None, :]
    c[:, C_ONES:C_ONES + P] = 1
    c[:, C_SLOTMASK:C_SLOTMASK + GH] = p[:, None] % GD // HD == np.arange(GH)
    c[:, C_BMASK:C_BMASK + BPT] = p[:, None] // PADN == np.arange(BPT)
    c[:, C_DMASK:C_DMASK + PADN] = p[:, None] % PADN == np.arange(PADN)
    c[:, C_VALID] = valid
    c[:, C_DOWN:C_DOWN + E] = E - np.arange(E)
    c[:, C_TILE:C_TILE + SLOT_TILES] = np.arange(SLOT_TILES)
    c[:, C_HMASK:C_HMASK + GD] = p[:, None] // PADN == np.arange(GD) // HD
    c[:, C_TOKEN:C_TOKEN + 2 * TILES] = np.tile(np.arange(TILES) * BPT, 2) + p[:, None] // PADN
    c[:, C_TOKEN + 2 * TILES:C_ROW] = p[:, None] % PADN
    c[:, C_ROW:C_ROW + P] = p
    return c


QT = 4
XPB = 4
BEFORE_ATTENTION = """a0 w0 b0 a1 w1 b1 c0 a2 d0 w2 e0 b2 c1 f0 a3 d1 w3 b3 e1 g0 c2 f1 h0 d2 g1 e2 c3 f2 h1 d3 g2 e3 f3
    h2 g3 s0 h3""".split()
AFTER_ATTENTION = """c0 c1 d0 c2 d1 e0 c3 d2 e1 f0 d3 e2 f1 g0 e3 f2 g1 h0 f3 g2 t0 h1 o0 g3 t1 h2 x0 o1 t2 h3 y0 x1 o2 t3 y1 x2
    o3 y2 x3 y3""".split()


def follow(order, steps):
    for step in order:
        if step[0] in steps:
            steps[step[0]](int(step[1]))


def tiles_of(q):
    return range(QT * q, QT * (q + 1))


class Chain:

    def __init__(self, eng, sem):
        self.eng, self.sem, self.base, self.n = eng, sem, 0, 0

    def add(self, ins):
        ins.then_inc(self.sem, 1)
        self.n += 1

    def wait(self):
        self.eng.wait_ge(self.sem, self.base + self.n)

    def __call__(self, ins):
        self.add(ins)
        self.wait()

    @contextmanager
    def loop(self, start, end, steps):
        before = self.base + self.n
        with self.eng.Fori(start, end) as i:
            self.base, self.n = before + (i - start) * steps, 0
            yield i
            assert self.n == steps, (self.n, steps)
        self.base, self.n = before + (end - start) * steps, 0


def build(nc, xp, wt, rows, attn_w, gate_w, gate_b, w1, b1, w2, b2, const_in, out):
    f32, bf16, i32, u32 = mybir.dt.float32, mybir.dt.bfloat16, mybir.dt.int32, mybir.dt.uint32
    ALU, ACT, AX = mybir.AluOpType, mybir.ActivationFunctionType, mybir.AxisListType

    xs = nc.dram_tensor("normed_rows", (TILES * P, D), f32).ap()
    out_rows = out.rearrange("b n d -> (b n) d")

    ctx = ExitStack()
    with ctx:
        def sb(name, shape, dt=f32):
            return ctx.enter_context(nc.sbuf_tensor(name, shape, dt))

        def sem(name):
            return ctx.enter_context(nc.semaphore(name))

        W1 = sb("W1", [P, E, KC, FF])
        W2 = sb("W2", [P, E, HC, D])
        H = sb("H", [P, TILES, D])
        X = sb("X", [P, TILES, D])
        CO = sb("CO", [P, C_ALL])
        IDB = sb("IDB", [P, P], bf16)
        W2flat = W2[:, :, :, :].rearrange("p e h d -> p (e h d)")
        at = [0]

        def carve(shape, dt=f32):
            n = int(np.prod(shape))
            words = n if dt == f32 else n // 2
            ap = W2flat[:, at[0]:at[0] + words]
            at[0] += words
            if dt != f32:
                ap = ap.bitcast(dt)
            names = "abcde"[:len(shape)]
            kw = dict(zip(names, shape))
            return ap if len(shape) == 1 else ap.rearrange(f"p ({' '.join(names)}) -> p {' '.join(names)}", **kw)

        WT = carve([5, D])
        XP = [carve([5, P]) for _ in range(XPB)]
        ROWS = carve([3, D])
        AW = carve([4, KC * D])
        TQK = carve([KC, 2, G, 2, GD], bf16)
        TV = carve([KC, D], bf16)
        QS = [carve([G, P], bf16) for _ in range(2)]
        KH = carve([G, P], bf16)
        KL = carve([G, P], bf16)
        KXH = [carve([G, GH, P], bf16) for _ in range(2)]
        KXL = [carve([G, GH, P], bf16) for _ in range(2)]
        S = carve([G * GH, PADN])
        PR = carve([G * GH, PADN])
        PT = carve([G, P])
        VX = [W2flat[:, u * BPT * G * (GD + GH):(u + 1) * BPT * G * (GD + GH)].rearrange(
            "p (b g c) -> p b g c", b=BPT, g=G) for u in range(2)]
        assert 2 * BPT * G * (GD + GH) <= 5 * D + XPB * 5 * P
        SIG = carve([TILES, PADN])
        DV = carve([TILES, BPT])
        SREP = carve([TILES * BPT])
        MX = carve([G * GH])
        RS = carve([G * GH])
        XQR = carve([KC, BPT, GH, PADN], bf16)
        assert at[0] <= E * HC * D
        QI = sb("QI", [P, TILES, D], bf16)
        TO = sb("TO", [P, KC, D], bf16)
        XQT = sb("XQT", [P, 2, KC, P], bf16)
        XT = sb("XT", [P, 2, KC, P])
        ST = sb("ST", [P, TILES, 6])
        MV = sb("MV", [P, 2, TILES])
        SM = sb("SM", [P, 11, TILES])
        AL = sb("AL", [P, 4, 4])
        GW = sb("GW", [P, KC, E])
        GB = sb("GB", [P, E])
        B1 = sb("B1", [P, E * HC])
        B2 = sb("B2", [P, E, D])
        R = sb("R", [P, 10, TILES, E])
        GATE = sb("GATE", [P, 2, TILES])
        SLOT = sb("SLOT", [P, 2, TILES])
        SLOTT = sb("SLOTT", [P, 2, TILES])
        ET = sb("ET", [P, SLOT_TILES, E])
        EF = sb("EF", [P, SLOT_TILES])
        EI = sb("EI", [P, SLOT_TILES], i32)
        ROW1 = QI[:, :, :].rearrange("p t d -> p (t d)").rearrange("p (k t r) -> p k t r", k=2, t=TILES)
        FACTS = 6
        TILE1 = X[:, :, :].rearrange("p t d -> p (t d)").bitcast(bf16)[:, 0:FACTS * 2 * TILES * SLOT_TILES].rearrange(
            "p (f k t s) -> p f k t s", f=FACTS, k=2, t=TILES)
        FACT = sb("FACT", [P, FACTS - 1, 2, TILES], bf16)
        REST = sb("REST", [P, 2, TILES])
        TAKE = sb("TAKE", [P, SLOT_TILES], u32)
        GIVE = sb("GIVE", [P, SLOT_TILES], u32)
        SGATE = sb("SGATE", [P, SLOT_TILES])
        SIDX = sb("SIDX", [P, 2, 2], u32)
        XG = sb("XG", [P, 2, D])
        XGT = sb("XGT", [P, 2, KC, P])
        HP = QI[:, :, :].rearrange("p t d -> p (t d)").bitcast(f32).rearrange("p (u h) -> p u h", u=2)
        HT = sb("HT", [P, HC, P])
        Y = sb("Y", [P, 2, D])

        PS = [ctx.enter_context(nc.psum_tensor(f"PS{i}", [P, 512], f32)) for i in range(8)]
        psT = PS[0][:, 0:KC * P].rearrange("p (k n) -> p k n", k=KC)
        psQ, psK = (PS[i][:, :].rearrange("p (g n) -> p g n", g=G) for i in (1, 2))
        psV = [PS[3 + j // 2][:, (j % 2) * D:(j % 2 + 1) * D] for j in range(BPT)]
        psS = PS[5]
        psPT = PS[6][:, :].rearrange("p (g n) -> p g n", g=G)
        psT2 = [PS[i][:, 0:KC * P].rearrange("p (k n) -> p k n", k=KC) for i in (0, 1)]
        psO = [PS[7][:, 0:D], PS[2][:, 0:D]]
        psM = [PS[3 + q][:, 0:QT] for q in range(TILES // QT)]
        psL = PS[3]
        psA = PS[7][:, 0:G * (GD + GH)].rearrange("p (g c) -> p g c", g=G)
        psE = [PS[1][:, 0:D], PS[2][:, 0:D]]

        s_const_in = sem("const_in")
        s_embed_w_in = sem("embed_w_in")
        s_attn_w_in = sem("attn_w_in")
        s_misc_in = sem("misc_in")
        s_w1_in = sem("w1_in")
        s_w2_in = sem("w2_in")
        s_idb = sem("idb")
        s_abs_sums = sem("abs_sums")
        s_abs_total = sem("abs_total")
        s_embedded = sem("embedded")
        s_biased = sem("biased")
        s_part_sums = sem("part_sums")
        s_batch_means = sem("batch_means")
        s_scale_diag = sem("scale_diag")
        s_scale_rep = sem("scale_rep")
        s_scales_read = sem("scales_read")
        s_quantised = sem("quantised")
        s_q_turned = sem("q_turned")
        s_qT = sem("qT")
        s_q_made = sem("q_made")
        s_k_made = sem("k_made")
        s_v_made = sem("v_made")
        s_q_hi = sem("q_hi")
        s_k_hi = sem("k_hi")
        s_q_split = sem("q_split")
        s_k_low = sem("k_low")
        s_k_spread = sem("k_spread")
        s_v_spread = sem("v_spread")
        s_scored = sem("scored")
        s_s_scaled = sem("s_scaled")
        s_s_centred = sem("s_centred")
        s_probs = sem("probs")
        s_p_turned = sem("p_turned")
        s_pT = sem("pT")
        s_mixed = sem("mixed")
        s_attended = sem("attended")
        s_o_made = sem("o_made")
        s_h_new = sem("h_new")
        s_x2T = sem("x2T")
        s_logits_made = sem("logits_made")
        s_logits_centred = sem("logits_centred")
        s_logits_exp = sem("logits_exp")
        s_picks = sem("picks")
        s_ranked = sem("ranked")
        s_experts_known = sem("experts_known")
        s_xg_turned = sem("xg_turned")
        s_xgT = sem("xgT")
        s_hidden = sem("hidden")
        s_hp_ready = sem("hp_ready")
        s_h_turned = sem("h_turned")
        s_hT = sem("hT")
        s_y_made = sem("y_made")
        s_y_ready = sem("y_ready")
        s_rows_out = sem("rows_out")
        s_residual_out = sem("residual_out")
        s_tile_hot = sem("tile_hot")
        s_row_hot = sem("row_hot")
        s_tables_made = sem("tables_made")
        s_tables_known = sem("tables_known")
        s_take_idx = sem("take_idx")
        s_give_idx = sem("give_idx")
        s_y_biased = sem("y_biased")
        s_y_added = sem("y_added")
        s_pool_waits = sem("pool_waits")
        s_cleared = sem("cleared")
        s_k_spread_high = sem("k_spread_high")
        s_s_max = sem("s_max")
        s_dve_step = sem("dve_step")
        s_xp_in = [sem(f"xp_in{u}") for u in range(XPB)]
        KINDS = ("token", "row", "batch", "batch2", "row2")
        s_var = {k: sem(f"var_{k}") for k in KINDS}
        s_dev = {k: sem(f"dev_{k}") for k in KINDS}
        s_factors = {k: sem(f"factors_{k}") for k in KINDS}
        s_normed = {k: sem(f"normed_{k}") for k in KINDS}
        s_tokens = sem("tokens")
        s_gamma_done = sem("gamma_done")
        s_to_int = sem("to_int")
        s_to_int_done = sem("to_int_done")
        s_o_turned = sem("o_turned")
        s_oT = sem("oT")
        s_x2_turned = sem("x2_turned")
        s_xg_in = [sem(f"xg_in{u}") for u in range(2)]

        def free(eng, semaphore, n):
            if not (isinstance(n, int) and n <= 0):
                eng.wait_ge(semaphore, n)

        def const(a, n):
            return CO[:, a:a + n]

        block = ctx.enter_context(nc.Block())

        @block.sync
        def _(eng):
            eng.dma_start(CO[:, :], const_in).then_inc(s_const_in, 16)
            eng.dma_start(WT, wt).then_inc(s_embed_w_in, 16)
            eng.dma_start(ROWS, rows).then_inc(s_embed_w_in, 16)
            for u in range(XPB):
                eng.dma_start(XP[u], xp[u]).then_inc(s_xp_in[u], 16)
            with eng.Fori(0, TILES // XPB - 1) as i:
                for u in range(XPB):
                    t = XPB * i + u
                    eng.wait_ge(s_embedded, t + 1)
                    eng.dma_start(XP[u], xp[bass.ds(t + XPB, 1)].rearrange("o p c n -> (o p) c n")).then_inc(s_xp_in[u], 16)
            for e in range(E):
                eng.dma_start(W1[:, e, :, :], w1[e].rearrange("(k p) h -> p k h", p=P)).then_inc(s_w1_in, 16)
            eng.dma_start(B2[:, :, :], b2).then_inc(s_w1_in, 16)

            eng.wait_ge(s_attended, TILES)
            for e in range(E // 2):
                eng.dma_start(W2[:, e, :, :], w2[e].rearrange("(h p) d -> p h d", p=P)).then_inc(s_w2_in, 16)
            xs4 = xs.rearrange("(t p) d -> p t d", p=P)
            for q in range(TILES // QT):
                eng.wait_ge(s_normed["row2"], q + 1)
                eng.dma_start(xs4[:, QT * q:QT * (q + 1), :], X[:, QT * q:QT * (q + 1), :]).then_inc(s_rows_out, 16)
            o4 = out.rearrange("(t j) n d -> j n t d", j=BPT)
            for j in range(BPT):
                eng.dma_start(o4[j], H[PADN * j:PADN * j + NP, :, :]).then_inc(s_residual_out, 16)
            for e in range(E // 2, E):
                eng.dma_start(W2[:, e, :, :], w2[e].rearrange("(h p) d -> p h d", p=P)).then_inc(s_w2_in, 16)

        @block.tensor
        def _(pe):
            mm = nc.tensor.matmul
            pe.wait_ge(s_const_in, 16)
            pe.wait_ge(s_embed_w_in, 32)

            def embed(q):
                for t in tiles_of(q):
                    pe.wait_ge(s_xp_in[t % XPB], 16 * (t // XPB + 1))
                    free(pe, s_biased, t - 1)
                    for k in range(5):
                        last = mm(psE[t % 2], XP[t % XPB][:, k, :], WT[:, k, :], start=k == 0, stop=k == 4)
                    last.then_inc(s_embedded, 1)

            def weight_sums(q):
                if q == 0:
                    pe.wait_ge(s_abs_sums, 1)
                    mm(PS[0][:, 0:4], const(C_ONES, P), AL[:, 0, :], start=True, stop=True).then_inc(s_abs_total, 1)

            means = [0]

            def batch_mean(q, row=0):
                means[0] += 1
                pe.wait_ge(s_part_sums, means[0])
                mm(psM[q], const(C_MEAN, P), SM[:, row, QT * q:QT * (q + 1)], start=True, stop=True).then_inc(s_batch_means, 1)

            follow(BEFORE_ATTENTION[:BEFORE_ATTENTION.index("s0")], {"a": embed, "w": weight_sums, "d": batch_mean})
            pe.wait_ge(s_scale_diag, 2)
            mm(PS[1][:, 0:TILES * BPT], const(C_REP, P), DV.rearrange("p t b -> p (t b)"), start=True, stop=True).then_inc(s_scale_rep, 1)
            mm(PS[2][:, :], const(C_SAME, P), SIG.rearrange("p t n -> p (t n)"), start=True, stop=True).then_inc(s_scale_rep, 1)

            def turn(t, ps):
                for k in range(KC):
                    last = mm(ps[:, k, :], QI[:, t, k * P:(k + 1) * P], IDB[:, :], start=True, stop=True)
                return last

            def turn_tile(t):
                free(pe, s_qT, t)
                turn(t, psT).then_inc(s_q_turned, 1)

            def project(t):
                pe.wait_ge(s_qT, t + 1)
                free(pe, s_q_split, t)
                for m, ps, done in ((0, psQ, s_q_made), (1, psK, s_k_made)):
                    if m:
                        free(pe, s_k_low, t)
                    for g in range(G):
                        for k in range(KC):
                            last = mm(ps[:, g, :], TQK[:, k, m, g, :, :], XQR[:, k, :, 0, :], start=k == 0, stop=k == KC - 1)
                    last.then_inc(done, 1)
                free(pe, s_v_spread, t)
                for j in range(BPT):
                    for k in range(KC):
                        keys = XQR[:, k, j, :, :].rearrange("p r n -> p (r n)")
                        last = mm(psV[j], keys, TV[:, k, :], start=k == 0, stop=k == KC - 1)
                last.then_inc(s_v_made, 1)

            def score(t, u):
                pe.wait_ge(s_q_split, t + 1)
                pe.wait_ge(s_k_spread, t + 1)
                pe.wait_ge(s_k_spread_high, t + 1)
                free(pe, s_s_scaled, t)
                for j in range(BPT):
                    r = slice(j * PADN, (j + 1) * PADN)
                    for g in range(G):
                        for part, kx in enumerate((KXH[u], KXL[u])):
                            last = mm(psS[r, g * P:(g + 1) * P], QS[u][:, g, r], kx[:, g, :, r], start=part == 0, stop=part == 1)
                last.then_inc(s_scored, 1)

            def mix(t, u):
                pe.wait_ge(s_probs, t + 1)
                free(pe, s_pT, t)
                for g in range(G):
                    last = nc.tensor.transpose(psPT[:, g, :], PR[:, g * GH:(g + 1) * GH, :].rearrange("p h n -> p (h n)"), const(C_IDENT, P))
                last.then_inc(s_p_turned, 1)
                pe.wait_ge(s_pT, t + 1)
                pe.wait_ge(s_v_spread, t + 1)
                free(pe, s_attended, t)
                for j in range(BPT):
                    r = slice(j * PADN, (j + 1) * PADN)
                    for g in range(G):
                        last = mm(psA[r, g, :], PT[:, g, r], VX[u][:, j, g, :], start=True, stop=True)
                last.then_inc(s_mixed, 1)

            def attention(t, u, first=False, ahead=2):
                if ahead >= 1:
                    project(t + 1)
                if ahead >= 2:
                    turn_tile(t + 2)
                score(t, u)
                if not first:
                    mix(t - 1, 1 - u)

            pe.wait_ge(s_quantised, TILES // QT)
            pe.wait_ge(s_scales_read, 1)
            pe.wait_ge(s_idb, 1)
            turn_tile(0)
            project(0)
            turn_tile(1)
            attention(0, 0, first=True)
            attention(1, 1)
            with pe.Fori(1, TILES // 2 - 1) as i:
                for u in range(2):
                    attention(2 * i + u, u)
            attention(TILES - 2, 0, ahead=1)
            attention(TILES - 1, 1, ahead=0)
            mix(TILES - 1, 1)

            copied = [None, None]

            def turn_out(t):
                if copied[t % 2]:
                    pe.wait_ge(*copied[t % 2])
                turn(t, psT2[t % 2]).then_inc(s_o_turned, 1)
                copied[t % 2] = s_oT, t + 1

            def project_out(q):
                pe.wait_ge(s_quantised, TILES // QT + q + 1)
                turn_out(QT * q)
                for t in tiles_of(q):
                    if t + 1 in tiles_of(q):
                        turn_out(t + 1)
                    pe.wait_ge(s_oT, t + 1)
                    free(pe, s_h_new, t - 1)
                    for k in range(KC):
                        last = mm(psO[t % 2], XQT[:, t % 2, k, :], TO[:, k, :], start=k == 0, stop=k == KC - 1)
                    last.then_inc(s_o_made, 1)

            def turn_rows(t):
                pe.wait_ge(*copied[t % 2])
                for k in range(KC):
                    last = nc.tensor.transpose(psT2[t % 2][:, k, :], X[:, t, k * P:(k + 1) * P], const(C_IDENT, P))
                last.then_inc(s_x2_turned, 1)
                copied[t % 2] = s_x2T, t + 1

            def logits(q):
                pe.wait_ge(s_misc_in, 48)
                pe.wait_ge(s_normed["row2"], q + 1)
                turn_rows(QT * q)
                for t in tiles_of(q):
                    if t + 1 in tiles_of(q):
                        turn_rows(t + 1)
                    pe.wait_ge(s_x2T, t + 1)
                    for k in range(KC):
                        last = mm(psL[:, t * E:(t + 1) * E], XT[:, t % 2, k, :], GW[:, k, :], start=k == 0, stop=k == KC - 1)
                    last.then_inc(s_logits_made, 1)

            follow(AFTER_ATTENTION, {"c": batch_mean, "d": lambda q: batch_mean(q, 1), "t": project_out, "y": logits})
            pe.wait_ge(s_picks, 1)
            oh = R[:, 0, :, :].rearrange("p t e -> p (t e)")
            mm(PS[1][:, 0:TILES * E], const(C_TRI, P), oh, start=True, stop=True).then_inc(s_ranked, 1)
            mm(PS[2][:, 0:TILES * E], const(C_ONES, P), oh, start=True, stop=True).then_inc(s_ranked, 1)

            pe.wait_ge(s_row_hot, 1)
            pe.wait_ge(s_tile_hot, FACTS)
            n = 0
            for k in range(2):
                for t in range(TILES):
                    last = mm(PS[3][:, 0:FACTS * SLOT_TILES], ROW1[:, k, t, :], TILE1[:, :, k, t, :],
                              start=n == 0, stop=n == 2 * TILES - 1)
                    n += 1
            last.then_inc(s_tables_made, 1)

            def expert(t):
                return pe.value_load(EI[0:1, bass.ds(t, 1)], min_val=0, max_val=E - 1)

            def turn_x(t, u, i):
                pe.wait_ge(s_xg_in[u], 16 * (i + 1))
                free(pe, s_xgT, t)
                for k in range(KC):
                    last = nc.tensor.transpose(psT[:, k, :], XG[:, u, k * P:(k + 1) * P], const(C_IDENT, P))
                last.then_inc(s_xg_turned, 1)

            def hidden(t, u):
                pe.wait_ge(s_xgT, t + 1)
                e = expert(t)
                free(pe, s_hp_ready, t - 1)
                for half in range(2):
                    for k in range(KC):
                        last = mm(PS[1 + 2 * u + half][:, :], XGT[:, u, k, :], W1[:, e, k, half * 512:(half + 1) * 512],
                                  start=k == 0, stop=k == KC - 1)
                last.then_inc(s_hidden, 1)

            def turn_h(t, u):
                pe.wait_ge(s_hp_ready, t + 1)
                free(pe, s_hT, t)
                for h in range(HC):
                    last = nc.tensor.transpose(PS[5 + h // 4][:, (h % 4) * P:(h % 4 + 1) * P],
                                               HP[:, u, h * P:(h + 1) * P], const(C_IDENT, P))
                last.then_inc(s_h_turned, 1)

            def output(t):
                e = expert(t)
                pe.wait_ge(s_hT, t + 1)
                free(pe, s_y_biased, t)
                for h in range(HC):
                    last = mm(PS[7][:, 0:D], HT[:, h, :], W2[:, e, h, :], start=h == 0, stop=h == HC - 1)
                last.then_inc(s_y_made, 1)

            pe.wait_ge(s_experts_known, 1)
            pe.wait_ge(s_w1_in, 16 * (E + 1))
            turn_x(0, 0, 0)
            hidden(0, 0)
            turn_x(1, 1, 0)
            pe.wait_ge(s_w2_in, 16 * E)

            def experts(i):
                for u in range(2):
                    t = 2 * i + u
                    turn_h(t, u)
                    hidden(t + 1, 1 - u)
                    turn_x(t + 2, u, i + 1)
                    output(t)

            experts(0)
            with pe.Fori(1, (SLOT_TILES - 3) // 2) as i:
                experts(i)
            for t in range(SLOT_TILES - 3, SLOT_TILES):
                turn_h(t, t % 2)
                if t + 1 < SLOT_TILES:
                    hidden(t + 1, (t + 1) % 2)
                if t + 2 < SLOT_TILES:
                    turn_x(t + 2, t % 2, t // 2 + 1)
                output(t)

        @block.scalar
        def _(act):
            act.dma_start(AW, attn_w).then_inc(s_attn_w_in, 16)
            act.dma_start(GW[:, :, :], gate_w).then_inc(s_misc_in, 16)
            act.dma_start(GB[:, :], gate_b).then_inc(s_misc_in, 16)
            act.dma_start(B1[:, :], b1).then_inc(s_misc_in, 16)

            def tile_col(row, t):
                return SM[:, row, t:t + 1]

            def root(kind):
                def step(q):
                    act.wait_ge(s_var[kind], q + 1)
                    nc.scalar.activation(SM[:, 3, QT * q:QT * (q + 1)], SM[:, 2, QT * q:QT * (q + 1)], ACT.Sqrt).then_inc(s_dev[kind], 1)
                return step

            def norm(kind, src):
                def step(q):
                    act.wait_ge(s_factors[kind], q + 1)
                    for t in tiles_of(q):
                        last = nc.scalar.activation(X[:, t, :], src[:, t, :], ACT.Identity, scale=tile_col(8, t), bias=tile_col(9, t))
                    last.then_inc(s_normed[kind], 1)
                return step

            def to_int_range(first):
                def step(q):
                    act.wait_ge(s_to_int, first + q + 1)
                    for t in tiles_of(q):
                        last = nc.scalar.activation(X[:, t, :], X[:, t, :], ACT.Copy, scale=tile_col(10, t))
                    last.then_inc(s_to_int_done, 1)
                return step

            follow(BEFORE_ATTENTION, {"a": root("token"), "b": norm("token", X), "c": root("row"), "e": root("batch"),
                                      "f": norm("batch", H), "g": to_int_range(0)})

            def turned(t):
                act.wait_ge(s_q_turned, t + 1)
                free(act, s_v_made, t)
                for k in range(KC):
                    last = nc.scalar.activation(
                        XQR[:, k], psT[:, k, :].rearrange("p (b n) -> p b n", b=BPT).unsqueeze(2).to_broadcast([P, BPT, GH, PADN]),
                        ACT.Copy)
                last.then_inc(s_qT, 1)

            def split(t, u):
                act.wait_ge(s_q_made, t + 1)
                free(act, s_scored, t - 1)
                nc.scalar.activation(QS[u], psQ, ACT.Copy).then_inc(s_q_hi, 1)
                act.wait_ge(s_k_made, t + 1)
                free(act, s_k_spread_high, t)
                free(act, s_k_low, t)
                nc.scalar.activation(KH, psK, ACT.Copy).then_inc(s_k_hi, 1)

            def take_probs(t):
                act.wait_ge(s_p_turned, t + 1)
                free(act, s_mixed, t)
                nc.scalar.activation(PT, psPT, ACT.Copy).then_inc(s_pT, 1)

            def exps(t):
                act.wait_ge(s_s_centred, t + 1)
                free(act, s_p_turned, t)
                nc.scalar.activation(PR[:, :, 0:NP], S[:, :, 0:NP], ACT.Exp).then_inc(s_probs, 1)

            def attention(t, u, first=False, ahead=2):
                if ahead >= 1:
                    split(t + 1, 1 - u)
                if ahead >= 2:
                    turned(t + 2)
                if not first:
                    take_probs(t - 1)
                exps(t)

            turned(0)
            split(0, 0)
            turned(1)
            act.wait_ge(s_cleared, 1)
            attention(0, 0, first=True)
            attention(1, 1)
            with act.Fori(1, TILES // 2 - 1) as i:
                for u in range(2):
                    attention(2 * i + u, u)
            attention(TILES - 2, 0, ahead=1)
            attention(TILES - 1, 1, ahead=0)
            take_probs(TILES - 1)
            def take_turned_out(q):
                for t in tiles_of(q):
                    act.wait_ge(s_o_turned, t + 1)
                    free(act, s_o_made, t - 1)
                    nc.scalar.activation(XQT[:, t % 2], psT2[t % 2], ACT.Copy).then_inc(s_oT, 1)

            def take_turned_rows(q):
                for t in tiles_of(q):
                    act.wait_ge(s_x2_turned, t + 1)
                    free(act, s_logits_made, t - 1)
                    nc.scalar.activation(XT[:, t % 2], psT2[t % 2], ACT.Copy).then_inc(s_x2T, 1)

            follow(AFTER_ATTENTION, {"e": root("batch2"), "f": norm("batch2", X), "g": to_int_range(TILES // QT),
                                     "t": take_turned_out, "o": root("row2"), "x": norm("row2", H), "y": take_turned_rows})
            act.wait_ge(s_logits_centred, 1)
            nc.scalar.activation(R[:, 1, :, :], R[:, 2, :, :], ACT.Exp).then_inc(s_logits_exp, 1)

            def take_x(t, u):
                act.wait_ge(s_xg_turned, t + 1)
                free(act, s_hidden, t - 1)
                nc.scalar.activation(XGT[:, u, :, :], psT, ACT.Copy).then_inc(s_xgT, 1)

            def relu(t):
                e = act.value_load(EI[0:1, bass.ds(t, 1)], min_val=0, max_val=E - 1)
                act.wait_ge(s_h_turned, t + 1)
                free(act, s_y_made, t)
                for h in range(HC):
                    last = nc.scalar.activation(HT[:, h, :], PS[5 + h // 4][:, (h % 4) * P:(h % 4 + 1) * P], ACT.Relu,
                                                bias=B1[:, bass.ds(e * HC + h, 1)])
                last.then_inc(s_hT, 1)

            act.wait_ge(s_experts_known, 1)
            take_x(0, 0)
            take_x(1, 1)

            def experts(i):
                for u in range(2):
                    relu(2 * i + u)
                    take_x(2 * i + u + 2, u)

            experts(0)
            with act.Fori(1, (SLOT_TILES - 3) // 2) as i:
                experts(i)
            for t in range(SLOT_TILES - 3, SLOT_TILES):
                relu(t)
                if t + 2 < SLOT_TILES:
                    take_x(t + 2, t % 2)

        @block.gpsimd
        def _(pool):
            def spread(t, u):
                pool.wait_ge(s_k_hi, t + 1)
                free(pool, s_scored, t - 1)
                pool.sem_inc(s_pool_waits, 1)
                for h in range(GH):
                    last = pool.tensor_scalar(KXH[u][:, :, h, :], KH, CO[:, C_SLOTMASK + h:C_SLOTMASK + h + 1], 0.0, ALU.mult, ALU.add)
                last.then_inc(s_k_spread_high, 1)

            def centre(t):
                pool.wait_ge(s_s_max, t + 1)
                pool.tensor_tensor(S[:, :, 0:NP], S[:, :, 0:NP], MX.unsqueeze(2).to_broadcast([P, G * GH, NP]),
                                   ALU.subtract).then_inc(s_s_centred, 1)

            def attention(t, u, ahead=1):
                if ahead:
                    spread(t + 1, 1 - u)
                centre(t)

            def scale_tokens(q):
                x, h = (a[:, QT * q:QT * (q + 1), :] for a in (X, H))
                pool.wait_ge(s_embed_w_in, 32)
                pool.wait_ge(s_normed["token"], q + 1)
                pool.tensor_tensor(x, x, ROWS[:, 1:2, :].to_broadcast([P, QT, D]), ALU.mult).then_inc(s_gamma_done, 1)
                pool.wait_ge(s_gamma_done, q + 1)
                pool.tensor_tensor(h, x, ROWS[:, 2:3, :].to_broadcast([P, QT, D]), ALU.add).then_inc(s_tokens, 1)

            follow(BEFORE_ATTENTION, {"b": scale_tokens})
            spread(0, 0)
            attention(0, 0)
            attention(1, 1)
            with pool.Fori(1, TILES // 2 - 1) as i:
                for u in range(2):
                    attention(2 * i + u, u)
            attention(TILES - 2, 0)
            attention(TILES - 1, 1, ahead=0)

            def gather(t, u):
                free(pool, s_xg_turned, t - 1)
                pool.sem_inc(s_pool_waits, 1)
                pool.tensor_copy(SIDX[:, 0, u:u + 1], TAKE[:, bass.ds(t, 1)]).then_inc(s_take_idx, 1)
                pool.wait_ge(s_take_idx, t + 1)
                pool.sem_inc(s_pool_waits, 1)
                pool.indirect_dma_start(XG[:, u, :], None, xs,
                                        bass.IndirectOffsetOnAxis(ap=SIDX[:, 0, u:u + 1], axis=0)).then_inc(s_xg_in[u], 16)

            def give(t, u):
                pool.tensor_copy(SIDX[:, 1, u:u + 1], GIVE[:, bass.ds(t, 1)]).then_inc(s_give_idx, 1)
                pool.wait_ge(s_give_idx, t + 1)
                pool.wait_ge(s_y_ready, t + 1)
                free(pool, s_y_added, 16 * t)
                pool.sem_inc(s_pool_waits, 1)
                pool.indirect_dma_start(out_rows, bass.IndirectOffsetOnAxis(ap=SIDX[:, 1, u:u + 1], axis=0), Y[:, u, :],
                                        None, bounds_check=B * NP - 1, oob_is_err=False,
                                        compute_op=ALU.add).then_inc(s_y_added, 16)

            pool.wait_ge(s_tables_known, 1)
            pool.wait_ge(s_rows_out, 16 * (TILES // QT))
            gather(0, 0)
            gather(1, 1)
            pool.wait_ge(s_residual_out, 16 * BPT)

            def experts(i):
                for u in range(2):
                    gather(2 * i + u + 2, u)
                    if not (isinstance(i, int) and i + u == 0):
                        give(2 * i + u - 1, 1 - u)

            experts(0)
            with pool.Fori(1, (SLOT_TILES - 3) // 2) as i:
                experts(i)
            for t in range(SLOT_TILES - 3, SLOT_TILES + 1):
                if t + 2 < SLOT_TILES:
                    gather(t + 2, t % 2)
                give(t - 1, (t - 1) % 2)
            pool.wait_ge(s_y_added, 16 * SLOT_TILES)

        @block.vector
        def _(dve):
            v = nc.vector
            step = Chain(dve, s_dve_step)
            MEAN, VAR = MV[:, 0, :], MV[:, 1, :]

            def col(i):
                return SM[:, i, :]

            means_asked = [0]

            def part(a, q):
                return a[:, QT * q:QT * (q + 1)]

            def moments(src, q, ask_mean=False):
                for t in tiles_of(q):
                    step.add(v.bn_stats(ST[:, t, :], src[:, t, :]))
                step.wait()
                st = ST[:, QT * q:QT * (q + 1), :]
                mean, var, m5 = part(MEAN, q), part(VAR, q), part(col(5), q)
                step.add(v.tensor_tensor(mean, st[:, :, 1], st[:, :, 4], ALU.add))
                step.add(v.tensor_tensor(m5, st[:, :, 1], st[:, :, 4], ALU.subtract))
                step(v.tensor_tensor(var, st[:, :, 2], st[:, :, 5], ALU.add))
                step.add(v.tensor_scalar(mean, mean, 0.5, None, ALU.mult))
                step(v.scalar_tensor_tensor(m5, m5, 0.25, m5, ALU.mult, ALU.mult))
                step(v.scalar_tensor_tensor(var, var, 1.0 / D, m5, ALU.mult, ALU.add))

            def ask_root(kind, q, var):
                v.tensor_scalar(part(col(2), q), var, EPS, None, ALU.add).then_inc(s_var[kind], 1)

            def inverse(kind, q, dst):
                c2, c3, c4, c5 = (part(col(i), q) for i in (2, 3, 4, 5))
                dve.wait_ge(s_var[kind], q + 1)
                dve.wait_ge(s_dev[kind], q + 1)
                step(v.reciprocal(c4, c3))
                step(v.tensor_tensor(c5, c4, c4, ALU.mult))
                step(v.tensor_tensor(c5, c5, c2, ALU.mult))
                step(v.tensor_scalar(c5, c5, -0.5, 1.5, ALU.mult, ALU.add))
                step(v.tensor_tensor(part(col(dst), q), c4, c5, ALU.mult))

            def factors(kind, q, mean):
                v.scalar_tensor_tensor(part(col(9), q), mean, -1.0, part(col(8), q), ALU.mult, ALU.mult).then_inc(s_factors[kind], 1)

            def ask_batch_mean(ins):
                ins.then_inc(s_part_sums, 1)
                means_asked[0] += 1
                return means_asked[0]

            asked = {}

            def to_int_factor(first, kind):
                def do(q):
                    dve.wait_ge(s_normed[kind], q + 1)
                    c5, c6, c8 = (part(col(i), q) for i in (5, 6, 8))
                    step(v.tensor_reduce(c5, X[:, QT * q:QT * (q + 1), :], AX.X, ALU.max, apply_absolute_value=True))
                    step(v.tensor_scalar(c5, c5, 1e-5, None, ALU.max))
                    step(v.reciprocal(c8, c5))
                    v.tensor_scalar(part(col(10), q), c8, 127.0, None, ALU.mult).then_inc(s_to_int, 1)
                    if first:
                        step.add(v.tensor_scalar(c6, c5, 1.0 / 127.0, AL[:, 1, 3:4], ALU.mult, ALU.mult))
                    else:
                        step.add(v.tensor_scalar(c6, c5, 1.0 / 127.0, None, ALU.mult))
                return do

            def round_int(first):
                def do(q):
                    x = X[:, QT * q:QT * (q + 1), :]
                    dve.wait_ge(s_to_int_done, first + q + 1)
                    step(v.tensor_scalar(x, x, -128.0, 127.0, ALU.max, ALU.min))
                    v.tensor_scalar(QI[:, QT * q:QT * (q + 1), :], x, MAGIC, -MAGIC, ALU.add, ALU.add).then_inc(s_quantised, 1)
                    if q == TILES // QT - 1:
                        dve.wait_ge(s_quantised, first + q + 1)
                return do

            awv = AW.rearrange("p m (k g c) -> p m k g c", k=KC, g=G)

            def ternary(part):
                if part == 0:
                    v.tensor_copy(IDB[:, :], const(C_IDENT, P)).then_inc(s_idb, 1)
                    dve.wait_ge(s_attn_w_in, 16)
                    v.tensor_reduce(AL[:, 0, :], AW, AX.X, ALU.add, apply_absolute_value=True).then_inc(s_abs_sums, 1)
                if part == 1:
                    dve.wait_ge(s_abs_total, 1)
                    step(v.tensor_scalar(AL[:, 1, :], PS[0][:, 0:4], 1.0 / (D * D), 1e-5, ALU.mult, ALU.max))
                    step(v.reciprocal(AL[:, 2, :], AL[:, 1, :]))
                    for m in range(4):
                        step.add(v.tensor_scalar(AW[:, m, :], AW[:, m, :], AL[:, 2, m:m + 1], MAGIC, ALU.mult, ALU.add))
                if part == 2:
                    step.wait()
                    step(v.tensor_scalar(AW, AW, -MAGIC, 1.0, ALU.add, ALU.min))
                    for k in range(KC):
                        step.add(v.tensor_scalar(TQK[:, k, 0, :, 0, :], awv[:, 0, k, :, :], -1.0, None, ALU.max))
                if part == 3:
                    for m in range(2):
                        for r in range(2):
                            for k in range(KC):
                                if m or r:
                                    step.add(v.tensor_scalar(TQK[:, k, m, :, r, :], awv[:, m, k, :, :], -1.0, None, ALU.max))
                    for m, dst in ((2, TV), (3, TO[:, :, :])):
                        step.add(v.tensor_scalar(dst, AW[:, m, :].rearrange("p (k c) -> p k c", k=KC), -1.0, None, ALU.max))
                    step.add(v.tensor_scalar(AL[:, 3, 0:1], AL[:, 1, 0:1], AL[:, 1, 1:2], HD ** -0.5, ALU.mult, ALU.mult))
                    v.memset(PR, 0.0).then_inc(s_cleared, 1)

            def token_moments(q):
                for t in tiles_of(q):
                    dve.wait_ge(s_embedded, t + 1)
                    v.tensor_tensor(X[:, t, :], psE[t % 2], ROWS[:, 0, :], ALU.add).then_inc(s_biased, 1)
                dve.wait_ge(s_biased, QT * (q + 1))
                moments(X, q)
                ask_root("token", q, part(VAR, q))

            def token_factors(q):
                inverse("token", q, 8)
                factors("token", q, part(MEAN, q))

            def row_moments(q):
                dve.wait_ge(s_tokens, q + 1)
                moments(H, q)
                ask_root("row", q, part(VAR, q))

            def normed_squares(q):
                inverse("row", q, 7)
                step(v.tensor_tensor(part(col(0), q), part(VAR, q), part(col(7), q), ALU.mult))
                asked[q] = ask_batch_mean(v.tensor_tensor(part(col(0), q), part(col(0), q), part(col(7), q), ALU.mult))

            def batch_root(kind):
                def do(q):
                    dve.wait_ge(s_batch_means, asked[q])
                    ask_root(kind, q, psM[q])
                return do

            def row_and_batch_factors(q):
                inverse("batch", q, 8)
                step(v.tensor_tensor(part(col(8), q), part(col(8), q), part(col(7), q), ALU.mult))
                factors("batch", q, part(MEAN, q))

            def scale_layouts(q):
                step.wait()
                v.tensor_tensor(DV, scale.to_broadcast([P, TILES, BPT]),
                                const(C_BMASK, BPT).unsqueeze(1).to_broadcast([P, TILES, BPT]), ALU.mult).then_inc(s_scale_diag, 1)
                v.tensor_tensor(SIG, scale.to_broadcast([P, TILES, PADN]),
                                const(C_DMASK, PADN).unsqueeze(1).to_broadcast([P, TILES, PADN]), ALU.mult).then_inc(s_scale_diag, 1)

            scale = SM[:, 6, :].unsqueeze(2)
            dve.wait_ge(s_const_in, 16)
            dve.wait_ge(s_embed_w_in, 32)
            follow(BEFORE_ATTENTION, {"a": token_moments, "w": ternary, "b": token_factors, "c": row_moments, "d": normed_squares,
                                      "e": batch_root("batch"), "f": row_and_batch_factors, "g": to_int_factor(0, "batch"),
                                      "s": scale_layouts, "h": round_int(0)})
            dve.wait_ge(s_scale_rep, 2)
            step(v.tensor_scalar(SREP, PS[1][:, 0:TILES * BPT], AL[:, 1, 2:3], None, ALU.mult))
            v.scalar_tensor_tensor(SIG, PS[2][:, :].rearrange("p (t n) -> p t n", t=TILES), AL[:, 3, 0:1],
                                   scale.to_broadcast([P, TILES, PADN]), ALU.mult, ALU.mult).then_inc(s_scales_read, 1)
            dve.wait_ge(s_scales_read, 1)

            def split(t, u):
                dve.wait_ge(s_q_hi, t + 1)
                v.tensor_tensor(QS[u][GD:P], psQ[GD:P], QS[u][GD:P], ALU.subtract).then_inc(s_q_split, 1)
                dve.wait_ge(s_k_hi, t + 1)
                free(dve, s_k_spread, t)
                v.tensor_tensor(KL, psK, KH, ALU.subtract).then_inc(s_k_low, 1)
                dve.wait_ge(s_k_low, t + 1)
                free(dve, s_scored, t - 1)
                for h in range(GH):
                    last = v.tensor_scalar(KXL[u][:, :, h, :], KL, CO[:, C_SLOTMASK + h:C_SLOTMASK + h + 1], None, ALU.mult)
                last.then_inc(s_k_spread, 1)

            def scale_scores(t):
                dve.wait_ge(s_scored, t + 1)
                free(dve, s_probs, t)
                v.tensor_tensor(S, psS[:, :].rearrange("p (h n) -> p h n", n=PADN),
                                SIG[:, bass.ds(t, 1), :].to_broadcast([P, G * GH, PADN]), ALU.mult).then_inc(s_s_scaled, 1)
                dve.wait_ge(s_s_scaled, t + 1)
                v.tensor_reduce(MX, S[:, :, 0:NP], AX.X, ALU.max).then_inc(s_s_max, 1)

            def attend(t):
                dve.wait_ge(s_mixed, t + 1)
                step(v.reciprocal(RS.rearrange("p (g h) -> p g h", g=G), psA[:, :, GD:GD + GH]))
                v.tensor_tensor(X[:, t, :].rearrange("p (g h d) -> p g h d", g=G, h=GH),
                                psA[:, :, 0:GD].rearrange("p g (h d) -> p g h d", h=GH),
                                RS.rearrange("p (g h) -> p g h", g=G).unsqueeze(3).to_broadcast([P, G, GH, HD]),
                                ALU.mult).then_inc(s_attended, 1)
                dve.wait_ge(s_attended, t + 1)

            def spread_v(t, u):
                dve.wait_ge(s_v_made, t + 1)
                for j in range(BPT):
                    last = v.scalar_tensor_tensor(
                        VX[u][:, j, :, 0:GD], psV[j].rearrange("p (g c) -> p g c", g=G), SREP[:, bass.ds(t * BPT + j, 1)],
                        const(C_HMASK, GD).unsqueeze(1).to_broadcast([P, G, GD]), ALU.mult, ALU.mult)
                last.then_inc(s_v_spread, 1)

            def attention(t, u, first=False, ahead=1):
                if ahead:
                    split(t + 1, 1 - u)
                scale_scores(t)
                if not first:
                    attend(t - 1)
                if ahead:
                    spread_v(t + 1, 1 - u)

            for u in range(2):
                for j in range(BPT):
                    step.add(v.tensor_copy(VX[u][:, j, :, GD:GD + GH],
                                           const(C_BMASK, BPT).unsqueeze(1).to_broadcast([P, G, GH])))
            step.wait()
            split(0, 0)
            spread_v(0, 0)
            attention(0, 0, first=True)
            attention(1, 1)
            with step.loop(1, TILES // 2 - 1, 2) as i:
                for u in range(2):
                    attention(2 * i + u, u)
            attention(TILES - 2, 0)
            attention(TILES - 1, 1, ahead=0)
            attend(TILES - 1)

            def out_mean(q):
                moments(X, q)
                asked[q] = ask_batch_mean(v.tensor_copy(part(col(0), q), part(MEAN, q)))

            def out_squares(q):
                dve.wait_ge(s_batch_means, asked[q])
                c5, c7 = part(col(5), q), part(col(7), q)
                step(v.tensor_copy(c7, psM[q]))
                step(v.tensor_tensor(c5, part(MEAN, q), c7, ALU.subtract))
                step(v.tensor_tensor(c5, c5, c5, ALU.mult))
                asked[q] = ask_batch_mean(v.tensor_tensor(part(col(1), q), c5, part(VAR, q), ALU.add))

            def out_factors(q):
                inverse("batch2", q, 8)
                factors("batch2", q, part(col(7), q))

            def add_attention(q):
                for t in tiles_of(q):
                    dve.wait_ge(s_o_made, t + 1)
                    v.scalar_tensor_tensor(H[:, t, :], psO[t % 2], SM[:, 6, t:t + 1], H[:, t, :], ALU.mult, ALU.add).then_inc(s_h_new, 1)
                dve.wait_ge(s_h_new, QT * (q + 1))
                moments(H, q)
                ask_root("row2", q, part(VAR, q))

            def row_factors(q):
                inverse("row2", q, 8)
                factors("row2", q, part(MEAN, q))

            follow(AFTER_ATTENTION, {"c": out_mean, "d": out_squares, "e": batch_root("batch2"), "f": out_factors,
                                     "g": to_int_factor(TILES // QT, "batch2"), "h": round_int(TILES // QT),
                                     "o": add_attention, "x": row_factors})
            dve.wait_ge(s_misc_in, 48)
            dve.wait_ge(s_logits_made, TILES)
            step(v.tensor_tensor(R[:, 1, :, :], psL[:, 0:TILES * E].rearrange("p (t e) -> p t e", e=E),
                                 GB[:, :].unsqueeze(1).to_broadcast([P, TILES, E]), ALU.add))

            def r(i):
                return R[:, i, :, :]

            def wide(i):
                return SM[:, i, :].unsqueeze(2).to_broadcast([P, TILES, E])

            down = const(C_DOWN, E).unsqueeze(1).to_broadcast([P, TILES, E])
            step(v.tensor_reduce(col(0), r(1), AX.X, ALU.max))
            v.tensor_tensor(r(2), r(1), wide(0), ALU.subtract).then_inc(s_logits_centred, 1)
            dve.wait_ge(s_logits_exp, 1)
            step(v.tensor_reduce(col(1), r(1), AX.X, ALU.add))
            step(v.reciprocal(col(1), col(1)))
            for k in range(2):
                step(v.tensor_reduce(col(0), r(1), AX.X, ALU.max))
                step.add(v.tensor_tensor(GATE[:, k, :], col(0), col(1), ALU.mult))
                step(v.tensor_tensor(r(2), r(1), wide(0), ALU.is_ge))
                step(v.tensor_tensor(r(2), r(2), down, ALU.mult))
                step(v.tensor_reduce(col(2), r(2), AX.X, ALU.max))
                step(v.tensor_tensor(r(3 + k), down, wide(2), ALU.is_equal))
                if k == 0:
                    step(v.scalar_tensor_tensor(r(1), r(3), -2.0, r(1), ALU.mult, ALU.add))
            step(v.tensor_tensor(r(0), r(3), r(4), ALU.add))
            v.tensor_scalar(r(0), r(0), CO[:, C_VALID:C_VALID + 1], None, ALU.mult).then_inc(s_picks, 1)
            dve.wait_ge(s_ranked, 2)
            step(v.tensor_copy(r(5), PS[2][:, 0:TILES * E].rearrange("p (t e) -> p t e", e=E)))
            a, b = 5, 6
            for d in (1, 2, 4, 8):
                step.add(v.tensor_copy(R[:, b, 0:d, :], R[:, a, 0:d, :]))
                step(v.tensor_tensor(R[:, b, d:, :], R[:, a, d:, :], R[:, a, 0:TILES - d, :], ALU.add))
                a, b = b, a
            count = R[:, a, TILES - 1, :]
            cum = R[:, 7, 0, :]
            cum2 = R[:, 7, 1, :]
            step(v.tensor_scalar(cum, count, 1.0 / P, (P - 1) / P - (P - 1) / (2 * P), ALU.mult, ALU.add))
            step(v.tensor_scalar(cum, cum, MAGIC, -MAGIC, ALU.add, ALU.add))
            step(v.tensor_copy(R[:, 7, 2, :], cum))
            x, y = 0, 1
            for d in (1, 2, 4):
                step.add(v.tensor_copy(R[:, 7, y, 0:d], R[:, 7, x, 0:d]))
                step(v.tensor_tensor(R[:, 7, y, d:], R[:, 7, x, d:], R[:, 7, x, 0:E - d], ALU.add))
                x, y = y, x
            step(v.tensor_tensor(R[:, 7, 2, :], R[:, 7, x, :], R[:, 7, 2, :], ALU.subtract))
            step(v.tensor_scalar(R[:, 7, 2, :], R[:, 7, 2, :], float(P), None, ALU.mult))
            step(v.tensor_tensor(ET[:, :, :], const(C_TILE, SLOT_TILES).unsqueeze(2).to_broadcast([P, SLOT_TILES, E]),
                                 R[:, 7, x:x + 1, :].to_broadcast([P, SLOT_TILES, E]), ALU.is_ge))
            step(v.tensor_reduce(EF[:, :], ET[:, :, :], AX.X, ALU.add))
            v.tensor_scalar(EI[:, :], EF[:, :], float(E - 1), None, ALU.min).then_inc(s_experts_known, 1)
            step(v.tensor_tensor(r(8), PS[1][:, 0:TILES * E].rearrange("p (t e) -> p t e", e=E),
                                 R[:, 7, 2:3, :].to_broadcast([P, TILES, E]), ALU.add))
            step(v.tensor_tensor(R[:, 8, 1:, :], R[:, 8, 1:, :], R[:, a, 0:TILES - 1, :], ALU.add))
            for k in range(2):
                step(v.tensor_tensor(r(9), r(8), r(3 + k), ALU.mult))
                step(v.tensor_reduce(SLOT[:, k, :], r(9), AX.X, ALU.add))
            step(v.tensor_scalar(SLOT[:, :, :], SLOT[:, :, :], 1.0, CO[:, C_VALID:C_VALID + 1], ALU.add, ALU.mult))
            step(v.tensor_scalar(SLOT[:, :, :], SLOT[:, :, :], -1.0, None, ALU.add))
            step(v.tensor_scalar(SLOTT[:, :, :], SLOT[:, :, :], 1.0 / P, -(P - 1) / (2 * P), ALU.mult, ALU.add))
            step(v.tensor_scalar(SLOTT[:, :, :], SLOTT[:, :, :], MAGIC, -MAGIC, ALU.add, ALU.add))
            step(v.scalar_tensor_tensor(SLOT[:, :, :], SLOTT[:, :, :], -float(P), SLOT[:, :, :], ALU.mult, ALU.add))
            step.add(v.tensor_copy(FACT[:, 0:2], const(C_TOKEN, 4 * TILES).rearrange("p (f k t) -> p f k t", f=2, k=2)))
            step(v.tensor_copy(FACT[:, 2], GATE[:, :, :]))
            step(v.tensor_tensor(REST[:, :, :], GATE[:, :, :], FACT[:, 2], ALU.subtract))
            step(v.tensor_copy(FACT[:, 3], REST[:, :, :]))
            step(v.tensor_tensor(FACT[:, 4], REST[:, :, :], FACT[:, 3], ALU.subtract))
            dve.wait_ge(s_rows_out, 16 * (TILES // QT))
            pairs = [P, 2 * TILES, SLOT_TILES]

            def flat(ap):
                return ap.rearrange("p k t -> p (k t)").unsqueeze(2)

            hot = TILE1[:, 0].rearrange("p k t s -> p (k t) s")
            v.tensor_tensor(hot, flat(SLOTT[:, :, :]).to_broadcast(pairs),
                            const(C_TILE, SLOT_TILES).unsqueeze(1).to_broadcast(pairs), ALU.is_equal).then_inc(s_tile_hot, 1)
            rows = [P, 2 * TILES, P]
            v.tensor_tensor(ROW1.rearrange("p k t r -> p (k t) r"), flat(SLOT[:, :, :]).to_broadcast(rows),
                            const(C_ROW, P).unsqueeze(1).to_broadcast(rows), ALU.is_equal).then_inc(s_row_hot, 1)
            dve.wait_ge(s_tile_hot, 1)
            for f in range(1, FACTS):
                v.tensor_tensor(TILE1[:, f].rearrange("p k t s -> p (k t) s"), hot, flat(FACT[:, f - 1]).to_broadcast(pairs),
                                ALU.mult).then_inc(s_tile_hot, 1)
            dve.wait_ge(s_tables_made, 1)
            step(v.tensor_copy(ET[:, :, 0:FACTS].rearrange("p s f -> p f s"),
                               PS[3][:, 0:FACTS * SLOT_TILES].rearrange("p (f s) -> p f s", f=FACTS)))
            step.add(v.scalar_tensor_tensor(TAKE[:, :], ET[:, :, 1], float(PADN), ET[:, :, 2], ALU.mult, ALU.add))
            step.add(v.tensor_tensor(SGATE[:, :], ET[:, :, 3], ET[:, :, 4], ALU.add))
            step(v.scalar_tensor_tensor(EF[:, :], ET[:, :, 1], float(NP), ET[:, :, 2], ALU.mult, ALU.add))
            step.add(v.tensor_tensor(SGATE[:, :], SGATE[:, :], ET[:, :, 5], ALU.add))
            step(v.tensor_scalar(EF[:, :], EF[:, :], float(BEYOND), None, ALU.add))
            v.scalar_tensor_tensor(GIVE[:, :], ET[:, :, 0], -float(BEYOND), EF[:, :], ALU.mult, ALU.add).then_inc(s_tables_known, 1)
            dve.wait_ge(s_tables_known, 1)

            def take_hidden(t, u):
                dve.wait_ge(s_hidden, t + 1)
                free(dve, s_h_turned, t - 1)
                for half in range(2):
                    last = v.tensor_copy(HP[:, u, half * 512:(half + 1) * 512], PS[1 + 2 * u + half][:, :])
                last.then_inc(s_hp_ready, 1)

            def take_y(t, u, i):
                e = dve.value_load(EI[0:1, bass.ds(t, 1)], min_val=0, max_val=E - 1)
                dve.wait_ge(s_y_made, t + 1)
                free(dve, s_y_added, 16 * (t - 1))
                v.tensor_tensor(Y[:, u, :], PS[7][:, 0:D], B2[:, e, :], ALU.add).then_inc(s_y_biased, 1)
                dve.wait_ge(s_y_biased, t + 1)
                v.tensor_scalar(Y[:, u, :], Y[:, u, :], SGATE[:, bass.ds(t, 1)], None, ALU.mult).then_inc(s_y_ready, 1)

            dve.wait_ge(s_experts_known, 1)
            take_hidden(0, 0)

            def experts(i):
                for u in range(2):
                    take_hidden(2 * i + u + 1, 1 - u)
                    take_y(2 * i + u, u, i)

            experts(0)
            with dve.Fori(1, (SLOT_TILES - 3) // 2) as i:
                experts(i)
            for t in range(SLOT_TILES - 3, SLOT_TILES):
                if t + 1 < SLOT_TILES:
                    take_hidden(t + 1, (t + 1) % 2)
                take_y(t, t % 2, t // 2)


def kernel(x, L0_tok_W, L0_tok_b, L0_tok_gamma, L0_tok_beta, L0_attn_w_q, L0_attn_w_k, L0_attn_w_v, L0_attn_w_o,
           L0_ffn_gate_w, L0_ffn_gate_b, L0_ffn_w1, L0_ffn_b1, L0_ffn_w2, L0_ffn_b2):
    import concourse.bacc as bacc
    from concourse.bass_utils import run_bass_kernel_spmd

    def wide(a):
        return np.broadcast_to(a, (P,) + a.shape)

    x = np.asarray(x)
    pixels = np.zeros((B, MELS, PF, PADN), x.dtype)
    for f in range(PF):
        pixels[:, :, f, :NP] = x[:, :, f:f + HOP * (NP - 1) + 1:HOP]
    xp = pixels.reshape(TILES, BPT, 5, P, PADN).transpose(0, 3, 2, 1, 4).reshape(TILES, P, 5, P)
    wt = np.asarray(L0_tok_W).reshape(5, P, D).transpose(1, 0, 2)
    attn = [np.asarray(a).T.reshape(KC, P, D).transpose(1, 0, 2).reshape(P, KC * D)
            for a in (L0_attn_w_q, L0_attn_w_k, L0_attn_w_v, L0_attn_w_o)]
    arrays = {
        "xp": xp, "wt": wt,
        "rows": wide(np.stack([np.asarray(a) for a in (L0_tok_b, L0_tok_gamma, L0_tok_beta)])),
        "attn_w": np.stack(attn, 1),
        "gate_w": np.asarray(L0_ffn_gate_w).T.reshape(KC, P, E).transpose(1, 0, 2),
        "gate_b": wide(np.asarray(L0_ffn_gate_b)),
        "w1": np.asarray(L0_ffn_w1),
        "b1": np.asarray(L0_ffn_b1).reshape(E * HC, P).T,
        "w2": np.asarray(L0_ffn_w2),
        "b2": wide(np.asarray(L0_ffn_b2)),
        "const": constants(),
    }
    arrays = {f"in_{k}": np.ascontiguousarray(a) for k, a in arrays.items()}
    nc = bacc.Bacc("TRN2", target_bir_lowering=False, num_devices=1)
    args = [nc.dram_tensor(k, a.shape, mybir.dt.from_np(a.dtype), kind="ExternalInput").ap() for k, a in arrays.items()]
    args.append(nc.dram_tensor("out", (B, NP, D), mybir.dt.float32, kind="ExternalOutput").ap())
    build(nc, *args)
    r = run_bass_kernel_spmd(nc, [arrays], core_ids=[0])
    return r.results[0]["out"]
```

```python
from contextlib import ExitStack, contextmanager

import numpy as np
import concourse.bass as bass
from concourse import mybir

B, MELS, FRAMES = 64, 80, 125
PF, HOP, NP = 8, 4, 30
D, NH, HD = 256, 16, 16
E, FF = 8, 1024
P = 128
PADN = 32
BPT = P // PADN
TILES = B // BPT
KC = D // P
HC = FF // P
G, GH = 4, 4
GD = GH * HD
SLOT_TILES = B * NP * 2 // P + E - 1
BEYOND = 4096
EPS = 1e-5
MAGIC = 1.5 * 2.0 ** 23

C_IDENT, C_MEAN, C_SAME, C_REP, C_TRI, C_ONES = (P * i for i in range(6))
C_SLOTMASK = 6 * P
C_BMASK = C_SLOTMASK + GH
C_DMASK = C_BMASK + BPT
C_VALID = C_DMASK + PADN
C_DOWN = C_VALID + 1
C_TILE = C_DOWN + E
C_TOKEN = C_TILE + SLOT_TILES
C_ROW = C_TOKEN + 2 * 2 * TILES
C_HMASK = C_ROW + P
C_ALL = C_HMASK + GD


def constants():
    p = np.arange(P)
    c = np.zeros((P, C_ALL), np.float32)
    same = p[:, None] // PADN == p[None, :] // PADN
    valid = p % PADN < NP
    c[:, C_IDENT:C_IDENT + P] = np.eye(P)
    c[:, C_MEAN:C_MEAN + P] = (same & valid[:, None]) / np.float32(NP)
    c[:, C_SAME:C_SAME + P] = same
    c[:, C_REP:C_REP + P] = p[:, None] % PADN == p[None, :] % PADN
    c[:, C_TRI:C_TRI + P] = p[:, None] < p[None, :]
    c[:, C_ONES:C_ONES + P] = 1
    c[:, C_SLOTMASK:C_SLOTMASK + GH] = p[:, None] % GD // HD == np.arange(GH)
    c[:, C_BMASK:C_BMASK + BPT] = p[:, None] // PADN == np.arange(BPT)
    c[:, C_DMASK:C_DMASK + PADN] = p[:, None] % PADN == np.arange(PADN)
    c[:, C_VALID] = valid
    c[:, C_DOWN:C_DOWN + E] = E - np.arange(E)
    c[:, C_TILE:C_TILE + SLOT_TILES] = np.arange(SLOT_TILES)
    c[:, C_HMASK:C_HMASK + GD] = p[:, None] // PADN == np.arange(GD) // HD
    c[:, C_TOKEN:C_TOKEN + 2 * TILES] = np.tile(np.arange(TILES) * BPT, 2) + p[:, None] // PADN
    c[:, C_TOKEN + 2 * TILES:C_ROW] = p[:, None] % PADN
    c[:, C_ROW:C_ROW + P] = p
    return c


QT = 4
AB = 3
WARM = 28
POOL_TILES = 2
DRAIN = (0, 1, 2)
POOL_HEADS = 1
XPB = 4
BEFORE_ATTENTION = """p0 p1 a0 w0 p2 b0 a1 b1 w1 c0 a2 p3 w2 d0 c1 e0 a3 b2 d1 c2 f0 e1 d2 w3 b3 g0 c3 f1 e2 h0 g1 v0 d3
    e3 f2 h1 g2 f3 h2 g3 s0 h3""".split()
AFTER_ATTENTION = """c0 c1 c2 d0 d1 c3 d2 e0 d3 e1 f0 f1 g0 e2 e3 f2 g1 h0 f3 g2 t0 h1 o0 h2 g3 t1 x0 o1 t2 h3 y0 x1 o2
    t3 y1 x2 o3 y2 y3 x3""".split()


def follow(order, steps):
    for step in order:
        if step[0] in steps:
            steps[step[0]](int(step[1]))


PE_ROUND = "project_v+1 project_qk+1 turn+2 turn_probs-1 score+0 mix-1"
ACT_ROUND = "high_q+1 high_k+1 turned+2 take_probs-1 exps+0"
DVE_ROUND = "spread_v+1 low_q+1 scale+0 attend-1 low_k+1"
POOL_ROUND = "centre+0 spread_low+1 spread+2"


def rounds(order, steps, loop, after=lambda n: None):
    order = [(steps[name], int(lead)) for name, lead in (w.replace("+", " ").replace("-", " -").split() for w in order.split())]
    leads = [lead for _, lead in order]
    start = AB - min(leads)
    turns = (TILES - max(leads) - start) // AB

    def do_round(base, n):
        for step, lead in order:
            if not isinstance(base, int):
                step(base + (n + lead), (n + lead) % AB)
            elif 0 <= base + n + lead < TILES:
                step(base + n + lead, (n + lead) % AB)

    for n in range(-max(leads), start):
        do_round(0, n)
    with loop(turns) as i:
        for n in range(start, start + AB):
            do_round(i * AB, n)
    for n in range(start + AB * turns, TILES - min(leads)):
        do_round(0, n)
        after(n - start - AB * turns)


def tiles_of(q):
    return range(QT * q, QT * (q + 1))


class Chain:

    def __init__(self, eng, sem):
        self.eng, self.sem, self.base, self.n = eng, sem, 0, 0

    def add(self, ins):
        ins.then_inc(self.sem, 1)
        self.n += 1

    def wait(self):
        self.eng.wait_ge(self.sem, self.base + self.n)

    def __call__(self, ins):
        self.add(ins)
        self.wait()

    @contextmanager
    def loop(self, start, end, steps):
        before = self.base + self.n
        with self.eng.Fori(start, end) as i:
            self.base, self.n = before + (i - start) * steps, 0
            yield i
            assert self.n == steps, (self.n, steps)
        self.base, self.n = before + (end - start) * steps, 0


def build(nc, xp, wt, rows, attn_w, gate_w, gate_b, w1, b1, w2, b2, const_in, out):
    f32, bf16, i32, u32 = mybir.dt.float32, mybir.dt.bfloat16, mybir.dt.int32, mybir.dt.uint32
    ALU, ACT, AX = mybir.AluOpType, mybir.ActivationFunctionType, mybir.AxisListType

    xs = nc.dram_tensor("normed_rows", (TILES * P, D), f32).ap()
    out_rows = out.rearrange("b n d -> (b n) d")

    ctx = ExitStack()
    with ctx:
        def sb(name, shape, dt=f32):
            return ctx.enter_context(nc.sbuf_tensor(name, shape, dt))

        def sem(name):
            return ctx.enter_context(nc.semaphore(name))

        W1 = sb("W1", [P, E, KC, FF])
        W2 = sb("W2", [P, E, HC, D])
        H = sb("H", [P, TILES, D])
        X = sb("X", [P, TILES, D])
        CO = sb("CO", [P, C_ALL])
        IDB = sb("IDB", [P, P], bf16)
        W2flat = W2[:, :, :, :].rearrange("p e h d -> p (e h d)")
        at = [0]

        def carve(shape, dt=f32):
            n = int(np.prod(shape))
            words = n if dt == f32 else n // 2
            ap = W2flat[:, at[0]:at[0] + words]
            at[0] += words
            if dt != f32:
                ap = ap.bitcast(dt)
            names = "abcde"[:len(shape)]
            kw = dict(zip(names, shape))
            return ap if len(shape) == 1 else ap.rearrange(f"p ({' '.join(names)}) -> p {' '.join(names)}", **kw)

        WT = carve([5, D])
        XP = [carve([5, P]) for _ in range(XPB)]
        ROWS = carve([3, D])
        AW_at = at[0]
        AW = carve([4, KC * D])
        TQK = carve([KC, 2, G, 2, GD], bf16)
        TV = carve([KC, D], bf16)
        QS = [carve([G, P], bf16) for _ in range(AB)]
        KH = carve([G, P], bf16)
        KL = carve([G, P], bf16)
        KXH = [carve([G, GH, P], bf16) for _ in range(AB - 1)]
        KXL = [carve([G, GH, P], bf16) for _ in range(AB - 1)]
        for n, bufs in enumerate((KXH, KXL)):
            last_at = AW_at + n * G * GH * P // 2
            bufs.append(W2flat[:, last_at:last_at + G * GH * P // 2].bitcast(bf16).rearrange("p (a b c) -> p a b c", a=G, b=GH))
        assert G * GH * P <= 4 * KC * D
        S = carve([G * GH, PADN])
        PR = carve([G * GH, PADN])
        PT = carve([G, P])
        VX = [W2flat[:, u * BPT * G * (GD + GH):(u + 1) * BPT * G * (GD + GH)].rearrange(
            "p (b g c) -> p b g c", b=BPT, g=G) for u in range(AB)]
        assert AB * BPT * G * (GD + GH) <= 5 * D + XPB * 5 * P
        SIG = carve([TILES, PADN])
        DV = carve([TILES, BPT])
        SREP = carve([TILES * BPT])
        MX = carve([G * GH])
        RS = carve([G * GH])
        XQR = carve([KC, BPT, GH, PADN], bf16)
        assert at[0] <= E * HC * D
        QI = sb("QI", [P, TILES, D], bf16)
        TO = sb("TO", [P, KC, D], bf16)
        XQT = sb("XQT", [P, 2, 2, KC, P], bf16)
        XT = sb("XT", [P, 2, 2, KC, P])
        ST = sb("ST", [P, TILES, 6])
        MV = sb("MV", [P, TILES, 2])
        SM = sb("SM", [P, 11, TILES])
        AL = sb("AL", [P, 4, 4])
        GW = sb("GW", [P, KC, E])
        GB = sb("GB", [P, E])
        B1 = sb("B1", [P, E * HC])
        B2 = sb("B2", [P, E, D])
        R = sb("R", [P, 10, TILES, E])
        GATE = sb("GATE", [P, 2, TILES])
        SLOT = sb("SLOT", [P, 2, TILES])
        SLOTT = sb("SLOTT", [P, 2, TILES])
        ET = sb("ET", [P, SLOT_TILES, E])
        EF = sb("EF", [P, SLOT_TILES])
        EI = sb("EI", [P, SLOT_TILES], i32)
        ROW1 = QI[:, :, :].rearrange("p t d -> p (t d)").rearrange("p (k t r) -> p k t r", k=2, t=TILES)
        FACTS, POOL_FACTS = 6, 3
        TILE1 = X[:, :, :].rearrange("p t d -> p (t d)").bitcast(bf16)[:, 0:FACTS * 2 * TILES * SLOT_TILES].rearrange(
            "p (f k t s) -> p f k t s", f=FACTS, k=2, t=TILES)
        FACT = sb("FACT", [P, FACTS - 1, 2, TILES], bf16)
        REST = sb("REST", [P, 2, TILES])
        TAKE = sb("TAKE", [P, SLOT_TILES], u32)
        GIVE = sb("GIVE", [P, SLOT_TILES], u32)
        SGATE = sb("SGATE", [P, SLOT_TILES])
        SIDX = sb("SIDX", [P, 2, 2], u32)
        XG = sb("XG", [P, 2, D])
        XGT = sb("XGT", [P, 2, KC, P])
        HP = QI[:, :, :].rearrange("p t d -> p (t d)").bitcast(f32).rearrange("p (u h) -> p u h", u=2)
        HT = sb("HT", [P, HC, P])
        Y = sb("Y", [P, 2, D])

        PS = [ctx.enter_context(nc.psum_tensor(f"PS{i}", [P, 512], f32)) for i in range(8)]
        psT = PS[0][:, 0:KC * P].rearrange("p (k n) -> p k n", k=KC)
        psQ, psK = (PS[i][:, :].rearrange("p (g n) -> p g n", g=G) for i in (1, 2))
        psV = [PS[3 + j // 2][:, (j % 2) * D:(j % 2 + 1) * D] for j in range(BPT)]
        psS = PS[5]
        psPT = PS[6][:, :].rearrange("p (g n) -> p g n", g=G)
        psT2 = [PS[i][:, :].rearrange("p (t k n) -> p t k n", t=2, k=KC) for i in (0, 1)]
        psO = [PS[7][:, 0:D], PS[2][:, 0:D]]
        psM = [PS[3 + q][:, 0:QT] for q in range(TILES // QT)]
        psL = PS[3]
        psA = PS[7][:, 0:G * (GD + GH)].rearrange("p (g c) -> p g c", g=G)
        psE = [PS[i][:, 0:D] for i in (1, 2, 0, 7)]

        s_const_in = sem("const_in")
        s_embed_w_in = sem("embed_w_in")
        s_attn_w_in = sem("attn_w_in")
        s_misc_in = sem("misc_in")
        s_w1_in = sem("w1_in")
        s_w2_in = sem("w2_in")
        s_idb = sem("idb")
        s_weights_scaled = sem("weights_scaled")
        s_weights_cut = sem("weights_cut")
        s_ternary = sem("ternary")
        s_ones = sem("ones")
        s_abs_sums = sem("abs_sums")
        s_abs_total = sem("abs_total")
        s_embedded = sem("embedded")
        s_biased = sem("biased")
        s_part_sums = sem("part_sums")
        s_batch_means = sem("batch_means")
        s_scale_diag = sem("scale_diag")
        s_scale_rep = sem("scale_rep")
        s_scales_read = sem("scales_read")
        s_quantised = sem("quantised")
        s_q_turned = sem("q_turned")
        s_qT = sem("qT")
        s_q_made = sem("q_made")
        s_k_made = sem("k_made")
        s_v_made = sem("v_made")
        s_q_hi = sem("q_hi")
        s_k_hi = sem("k_hi")
        s_q_split = sem("q_split")
        s_k_low = sem("k_low")
        s_k_spread = sem("k_spread")
        s_v_spread = sem("v_spread")
        s_scored = sem("scored")
        s_s_scaled = sem("s_scaled")
        s_s_centred = sem("s_centred")
        s_probs = sem("probs")
        s_p_turned = sem("p_turned")
        s_pT = sem("pT")
        s_mixed = sem("mixed")
        s_attended = sem("attended")
        s_o_made = sem("o_made")
        s_h_new = sem("h_new")
        s_x2T = sem("x2T")
        s_logits_made = sem("logits_made")
        s_logits_centred = sem("logits_centred")
        s_logits_exp = sem("logits_exp")
        s_picks = sem("picks")
        s_ranked = sem("ranked")
        s_experts_known = sem("experts_known")
        s_xg_turned = sem("xg_turned")
        s_xgT = sem("xgT")
        s_hidden = sem("hidden")
        s_hp_ready = sem("hp_ready")
        s_h_turned = sem("h_turned")
        s_hT = sem("hT")
        s_y_made = sem("y_made")
        s_y_ready = sem("y_ready")
        s_rows_out = sem("rows_out")
        s_residual_out = sem("residual_out")
        s_tile_hot = sem("tile_hot")
        s_row_hot = sem("row_hot")
        s_tables_made = sem("tables_made")
        s_facts_hot = sem("facts_hot")
        s_pool_facts_hot = sem("pool_facts_hot")
        s_gate_parts = sem("gate_parts")
        s_warmed = sem("warmed")
        s_tables_known = sem("tables_known")
        s_take_idx = sem("take_idx")
        s_give_idx = sem("give_idx")
        s_y_biased = sem("y_biased")
        s_y_added = sem("y_added")
        s_pool_waits = sem("pool_waits")
        s_cleared = sem("cleared")
        s_exp_loaded = sem("exp_loaded")
        s_k_spread_high = sem("k_spread_high")
        s_k_spread_low = sem("k_spread_low")
        s_s_max = sem("s_max")
        s_dve_step = sem("dve_step")
        s_xp_in = [sem(f"xp_in{u}") for u in range(XPB)]
        KINDS = ("token", "row", "batch", "batch2", "row2")
        s_var = {k: sem(f"var_{k}") for k in KINDS}
        s_dev = {k: sem(f"dev_{k}") for k in KINDS}
        s_factors = {k: sem(f"factors_{k}") for k in KINDS}
        s_normed = {k: sem(f"normed_{k}") for k in KINDS}
        s_rows_in = sem("rows_in")
        s_copied = sem("copied")
        s_to_int = sem("to_int")
        s_to_int_done = sem("to_int_done")
        s_to_int_pool = sem("to_int_pool")
        s_o_turned = sem("o_turned")
        s_oT = sem("oT")
        s_x2_turned = sem("x2_turned")
        s_xg_in = [sem(f"xg_in{u}") for u in range(2)]

        def free(eng, semaphore, n):
            if not (isinstance(n, int) and n <= 0):
                eng.wait_ge(semaphore, n)

        def const(a, n):
            return CO[:, a:a + n]

        block = ctx.enter_context(nc.Block())

        @block.sync
        def _(eng):
            eng.dma_start(WT, wt).then_inc(s_embed_w_in, 16)
            eng.dma_start(XP[0], xp[0]).then_inc(s_xp_in[0], 16)
            eng.dma_start(ROWS, rows).then_inc(s_rows_in, 16)
            for u in range(1, XPB):
                eng.dma_start(XP[u], xp[u]).then_inc(s_xp_in[u], 16)
            eng.dma_start(CO[:, :], const_in).then_inc(s_const_in, 16)
            eng.dma_start(AW, attn_w).then_inc(s_attn_w_in, 16)
            eng.dma_start(GW[:, :, :], gate_w).then_inc(s_misc_in, 16)
            eng.dma_start(GB[:, :], gate_b).then_inc(s_misc_in, 16)
            eng.dma_start(B1[:, :], b1).then_inc(s_misc_in, 16)
            with eng.Fori(0, TILES // XPB - 1) as i:
                for u in range(XPB):
                    t = XPB * i + u
                    eng.wait_ge(s_embedded, t + 1)
                    eng.dma_start(XP[u], xp[bass.ds(t + XPB, 1)].rearrange("o p c n -> (o p) c n")).then_inc(s_xp_in[u], 16)
            for e in range(E):
                eng.dma_start(W1[:, e, :, :], w1[e].rearrange("(k p) h -> p k h", p=P)).then_inc(s_w1_in, 16)
            eng.dma_start(B2[:, :, :], b2).then_inc(s_w1_in, 16)

            eng.wait_ge(s_attended, TILES)
            for e in range(E // 2):
                eng.dma_start(W2[:, e, :, :], w2[e].rearrange("(h p) d -> p h d", p=P)).then_inc(s_w2_in, 16)
            xs4 = xs.rearrange("(t p) d -> p t d", p=P)
            for q in range(TILES // QT):
                eng.wait_ge(s_normed["row2"], q + 1)
                eng.dma_start(xs4[:, QT * q:QT * (q + 1), :], X[:, QT * q:QT * (q + 1), :]).then_inc(s_rows_out, 16)
            o4 = out.rearrange("(t j) n d -> j n t d", j=BPT)
            for j in range(BPT):
                eng.dma_start(o4[j], H[PADN * j:PADN * j + NP, :, :]).then_inc(s_residual_out, 16)
            for e in range(E // 2, E):
                eng.dma_start(W2[:, e, :, :], w2[e].rearrange("(h p) d -> p h d", p=P)).then_inc(s_w2_in, 16)

        @block.tensor
        def _(pe):
            mm = nc.tensor.matmul
            pe.wait_ge(s_embed_w_in, 16)

            def embed(q):
                for t in tiles_of(q):
                    pe.wait_ge(s_xp_in[t % XPB], 16 * (t // XPB + 1))
                    free(pe, s_copied, t - 3)
                    for k in range(5):
                        last = mm(psE[t % 4], XP[t % XPB][:, k, :], WT[:, k, :], start=k == 0, stop=k == 4)
                    last.then_inc(s_embedded, 1)

            def weight_sums(q):
                if q == 0:
                    pe.wait_ge(s_const_in, 16)
                    pe.wait_ge(s_abs_sums, 1)
                    mm(PS[6][:, 0:4], const(C_ONES, P), AL[:, 0, :], start=True, stop=True).then_inc(s_abs_total, 1)

            means = [0]

            def batch_mean(q, row=0):
                means[0] += 1
                pe.wait_ge(s_part_sums, means[0])
                mm(psM[q], const(C_MEAN, P), SM[:, row, QT * q:QT * (q + 1)], start=True, stop=True).then_inc(s_batch_means, 1)

            follow(BEFORE_ATTENTION[:BEFORE_ATTENTION.index("s0")], {"p": embed, "w": weight_sums, "d": batch_mean})
            pe.wait_ge(s_scale_diag, 2)
            mm(PS[6][:, 0:TILES * BPT], const(C_REP, P), DV.rearrange("p t b -> p (t b)"), start=True, stop=True).then_inc(s_scale_rep, 1)
            mm(PS[5][:, :], const(C_SAME, P), SIG.rearrange("p t n -> p (t n)"), start=True, stop=True).then_inc(s_scale_rep, 1)

            def turn(t, ps):
                for k in range(KC):
                    last = mm(ps[:, k, :], QI[:, t, k * P:(k + 1) * P], IDB[:, :], start=True, stop=True)
                return last

            def turn_tile(t, u):
                if isinstance(t, int):
                    pe.wait_ge(s_quantised, t // QT + 1)
                free(pe, s_qT, t)
                turn(t, psT).then_inc(s_q_turned, 1)

            def project_qk(t, u):
                pe.wait_ge(s_qT, t + 1)
                free(pe, s_q_split, t)
                for m, ps, done in ((0, psQ, s_q_made), (1, psK, s_k_made)):
                    if m:
                        free(pe, s_k_low, t)
                    for g in range(G):
                        for k in range(KC):
                            last = mm(ps[:, g, :], TQK[:, k, m, g, :, :], XQR[:, k, :, 0, :], start=k == 0, stop=k == KC - 1)
                    last.then_inc(done, 1)

            def project_v(t, u):
                pe.wait_ge(s_qT, t + 1)
                free(pe, s_v_spread, t)
                for j in range(BPT):
                    for k in range(KC):
                        keys = XQR[:, k, j, :, :].rearrange("p r n -> p (r n)")
                        last = mm(psV[j], keys, TV[:, k, :], start=k == 0, stop=k == KC - 1)
                last.then_inc(s_v_made, 1)

            def score(t, u):
                pe.wait_ge(s_q_split, t + 1)
                pe.wait_ge(s_k_spread, t + 1)
                pe.wait_ge(s_k_spread_low, t + 1)
                pe.wait_ge(s_k_spread_high, t + 1)
                free(pe, s_s_scaled, t)
                for j in range(BPT):
                    r = slice(j * PADN, (j + 1) * PADN)
                    for g in range(G):
                        for part, kx in enumerate((KXH[u], KXL[u])):
                            last = mm(psS[r, g * P:(g + 1) * P], QS[u][:, g, r], kx[:, g, :, r], start=part == 0, stop=part == 1)
                last.then_inc(s_scored, 1)

            def turn_probs(t, u):
                pe.wait_ge(s_probs, t + 1)
                free(pe, s_pT, t)
                for g in range(G):
                    last = nc.tensor.transpose(psPT[:, g, :], PR[:, g * GH:(g + 1) * GH, :].rearrange("p h n -> p (h n)"), const(C_IDENT, P))
                last.then_inc(s_p_turned, 1)

            def mix(t, u):
                pe.wait_ge(s_pT, t + 1)
                pe.wait_ge(s_v_spread, t + 1)
                free(pe, s_attended, t)
                for j in range(BPT):
                    r = slice(j * PADN, (j + 1) * PADN)
                    for g in range(G):
                        last = mm(psA[r, g, :], PT[:, g, r], VX[u][:, j, g, :], start=True, stop=True)
                last.then_inc(s_mixed, 1)

            pe.wait_ge(s_idb, 1)
            pe.wait_ge(s_ternary, 1)
            pe.wait_ge(s_ones, 1)
            def all_quantised(turns):
                pe.wait_ge(s_quantised, TILES // QT)
                return pe.Fori(0, turns)

            rounds(PE_ROUND, {"project_qk": project_qk, "project_v": project_v, "turn": turn_tile, "score": score,
                              "turn_probs": turn_probs, "mix": mix}, all_quantised)

            copied = [None, None]

            def turn_out(pair):
                if copied[pair % 2]:
                    pe.wait_ge(*copied[pair % 2])
                for t in range(2):
                    last = turn(2 * pair + t, psT2[pair % 2][:, t])
                last.then_inc(s_o_turned, 1)
                copied[pair % 2] = s_oT, pair + 1

            def project_out(q):
                pe.wait_ge(s_quantised, TILES // QT + q + 1)
                turn_out(2 * q)
                turn_out(2 * q + 1)
                for t in tiles_of(q):
                    pe.wait_ge(s_oT, t // 2 + 1)
                    free(pe, s_h_new, t - 1)
                    for k in range(KC):
                        last = mm(psO[t % 2], XQT[:, t // 2 % 2, t % 2, k, :], TO[:, k, :], start=k == 0, stop=k == KC - 1)
                    last.then_inc(s_o_made, 1)

            def turn_rows(pair):
                pe.wait_ge(*copied[pair % 2])
                for t in range(2):
                    for k in range(KC):
                        last = nc.tensor.transpose(psT2[pair % 2][:, t, k, :], X[:, 2 * pair + t, k * P:(k + 1) * P], const(C_IDENT, P))
                last.then_inc(s_x2_turned, 1)
                copied[pair % 2] = s_x2T, pair + 1

            def logits(q):
                pe.wait_ge(s_misc_in, 48)
                pe.wait_ge(s_normed["row2"], q + 1)
                turn_rows(2 * q)
                turn_rows(2 * q + 1)
                for t in tiles_of(q):
                    pe.wait_ge(s_x2T, t // 2 + 1)
                    for k in range(KC):
                        last = mm(psL[:, t * E:(t + 1) * E], XT[:, t // 2 % 2, t % 2, k, :], GW[:, k, :], start=k == 0, stop=k == KC - 1)
                    last.then_inc(s_logits_made, 1)

            follow(AFTER_ATTENTION, {"c": batch_mean, "d": lambda q: batch_mean(q, 1), "t": project_out, "y": logits})
            pe.wait_ge(s_picks, 1)
            oh = R[:, 0, :, :].rearrange("p t e -> p (t e)")
            mm(PS[1][:, 0:TILES * E], const(C_TRI, P), oh, start=True, stop=True).then_inc(s_ranked, 1)
            mm(PS[2][:, 0:TILES * E], const(C_ONES, P), oh, start=True, stop=True).then_inc(s_ranked, 1)

            n = 0
            for k in range(2):
                pe.wait_ge(s_row_hot, k + 1)
                pe.wait_ge(s_tile_hot, k + 1)
                pe.wait_ge(s_facts_hot, (k + 1) * (FACTS - POOL_FACTS - 1))
                pe.wait_ge(s_pool_facts_hot, (k + 1) * POOL_FACTS)
                for t in range(TILES):
                    last = mm(PS[3][:, 0:FACTS * SLOT_TILES], ROW1[:, k, t, :], TILE1[:, :, k, t, :],
                              start=n == 0, stop=n == 2 * TILES - 1)
                    n += 1
            last.then_inc(s_tables_made, 1)
            for n in range(WARM):
                last = mm(PS[6][:, 0:P], const(C_IDENT, P), const(C_IDENT, P), start=n == 0, stop=n == WARM - 1)
            last.then_inc(s_warmed, 1)

            def expert(t):
                return pe.value_load(EI[0:1, bass.ds(t, 1)], min_val=0, max_val=E - 1)

            def turn_x(t, u, i):
                pe.wait_ge(s_xg_in[u], 16 * (i + 1))
                free(pe, s_xgT, t)
                for k in range(KC):
                    last = nc.tensor.transpose(psT[:, k, :], XG[:, u, k * P:(k + 1) * P], const(C_IDENT, P))
                last.then_inc(s_xg_turned, 1)

            def hidden(t, u):
                e = expert(t)
                pe.wait_ge(s_xgT, t + 1)
                free(pe, s_hp_ready, t - 1)
                for half in range(2):
                    for k in range(KC):
                        last = mm(PS[1 + 2 * u + half][:, :], XGT[:, u, k, :], W1[:, e, k, half * 512:(half + 1) * 512],
                                  start=k == 0, stop=k == KC - 1)
                last.then_inc(s_hidden, 1)

            def turn_h(t, u):
                pe.wait_ge(s_hp_ready, t + 1)
                free(pe, s_hT, t)
                for h in range(HC):
                    last = nc.tensor.transpose(PS[5 + h // 4][:, (h % 4) * P:(h % 4 + 1) * P],
                                               HP[:, u, h * P:(h + 1) * P], const(C_IDENT, P))
                last.then_inc(s_h_turned, 1)

            def output(t):
                e = expert(t)
                pe.wait_ge(s_hT, t + 1)
                free(pe, s_y_biased, t)
                for h in range(HC):
                    last = mm(PS[7][:, 0:D], HT[:, h, :], W2[:, e, h, :], start=h == 0, stop=h == HC - 1)
                last.then_inc(s_y_made, 1)

            pe.wait_ge(s_experts_known, 1)
            pe.wait_ge(s_w1_in, 16 * (E + 1))
            turn_x(0, 0, 0)
            hidden(0, 0)
            turn_x(1, 1, 0)
            pe.wait_ge(s_w2_in, 16 * E)

            def experts(i):
                for u in range(2):
                    t = 2 * i + u
                    turn_h(t, u)
                    hidden(t + 1, 1 - u)
                    turn_x(t + 2, u, i + 1)
                    output(t)

            experts(0)
            with pe.Fori(1, (SLOT_TILES - 3) // 2) as i:
                experts(i)
            for t in range(SLOT_TILES - 3, SLOT_TILES):
                turn_h(t, t % 2)
                if t + 1 < SLOT_TILES:
                    hidden(t + 1, (t + 1) % 2)
                if t + 2 < SLOT_TILES:
                    turn_x(t + 2, t % 2, t // 2 + 1)
                output(t)

        @block.scalar
        def _(act):

            def tile_col(row, t):
                return SM[:, row, t:t + 1]

            def root(kind):
                def step(q):
                    act.wait_ge(s_var[kind], q + 1)
                    nc.scalar.activation(SM[:, 3, QT * q:QT * (q + 1)], SM[:, 2, QT * q:QT * (q + 1)], ACT.Sqrt).then_inc(s_dev[kind], 1)
                return step

            def norm(kind, src):
                def step(q):
                    act.wait_ge(s_factors[kind], q + 1)
                    for t in tiles_of(q):
                        last = nc.scalar.activation(X[:, t, :], src[:, t, :], ACT.Identity, scale=tile_col(8, t), bias=tile_col(9, t))
                    last.then_inc(s_normed[kind], 1)
                return step

            def to_int_range(first, tiles):
                def step(q):
                    act.wait_ge(s_to_int, first + q + 1)
                    for t in tiles_of(q)[:tiles]:
                        last = nc.scalar.activation(X[:, t, :], X[:, t, :], ACT.Copy, scale=tile_col(10, t))
                    last.then_inc(s_to_int_done, 1)
                return step

            def copy_tokens(q):
                for t in tiles_of(q):
                    act.wait_ge(s_embedded, t + 1)
                    nc.scalar.activation(X[:, t, :], psE[t % 4], ACT.Copy).then_inc(s_copied, 1)

            follow(BEFORE_ATTENTION, {"p": copy_tokens, "a": root("token"), "c": root("row"), "e": root("batch"),
                                      "f": norm("batch", H), "g": to_int_range(0, QT)})

            def turned(t, u):
                act.wait_ge(s_q_turned, t + 1)
                free(act, s_v_made, t)
                free(act, s_k_made, t)
                for k in range(KC):
                    last = nc.scalar.activation(
                        XQR[:, k], psT[:, k, :].rearrange("p (b n) -> p b n", b=BPT).unsqueeze(2).to_broadcast([P, BPT, GH, PADN]),
                        ACT.Copy)
                last.then_inc(s_qT, 1)

            def high_q(t, u):
                act.wait_ge(s_q_made, t + 1)
                free(act, s_scored, t - 2)
                nc.scalar.activation(QS[u], psQ, ACT.Copy).then_inc(s_q_hi, 1)

            def high_k(t, u):
                act.wait_ge(s_k_made, t + 1)
                free(act, s_k_spread_high, t)
                free(act, s_k_low, t)
                nc.scalar.activation(KH, psK, ACT.Copy).then_inc(s_k_hi, 1)

            def take_probs(t, u):
                act.wait_ge(s_p_turned, t + 1)
                free(act, s_mixed, t)
                nc.scalar.activation(PT, psPT, ACT.Copy).then_inc(s_pT, 1)

            def exps(t, u):
                act.wait_ge(s_s_centred, t + 1)
                free(act, s_p_turned, t)
                nc.scalar.activation(PR[:, :, 0:NP], S[:, :, 0:NP], ACT.Exp).then_inc(s_probs, 1)

            act.wait_ge(s_dev["batch"], TILES // QT)
            nc.scalar.activation(R[:, 9, 0, 0:1], SM[:, 3, 0:1], ACT.Exp).then_inc(s_exp_loaded, 1)
            act.wait_ge(s_cleared, 1)
            rounds(ACT_ROUND, {"high_q": high_q, "high_k": high_k, "turned": turned, "take_probs": take_probs, "exps": exps},
                   lambda n: act.Fori(0, n))

            def take_turned_out(q):
                for pair in (2 * q, 2 * q + 1):
                    act.wait_ge(s_o_turned, pair + 1)
                    free(act, s_o_made, 2 * pair - 2)
                    nc.scalar.activation(XQT[:, pair % 2], psT2[pair % 2], ACT.Copy).then_inc(s_oT, 1)

            def take_turned_rows(q):
                for pair in (2 * q, 2 * q + 1):
                    act.wait_ge(s_x2_turned, pair + 1)
                    free(act, s_logits_made, 2 * pair - 2)
                    nc.scalar.activation(XT[:, pair % 2], psT2[pair % 2], ACT.Copy).then_inc(s_x2T, 1)

            follow(AFTER_ATTENTION, {"e": root("batch2"), "f": norm("batch2", X), "g": to_int_range(TILES // QT, QT - POOL_TILES),
                                     "t": take_turned_out, "o": root("row2"), "y": take_turned_rows})
            act.wait_ge(s_logits_centred, 1)
            nc.scalar.activation(R[:, 1, :, :], R[:, 2, :, :], ACT.Exp).then_inc(s_logits_exp, 1)

            def take_x(t, u):
                act.wait_ge(s_xg_turned, t + 1)
                free(act, s_hidden, t - 1)
                nc.scalar.activation(XGT[:, u, :, :], psT, ACT.Copy).then_inc(s_xgT, 1)

            def relu(t):
                e = act.value_load(EI[0:1, bass.ds(t, 1)], min_val=0, max_val=E - 1)
                act.wait_ge(s_h_turned, t + 1)
                free(act, s_y_made, t)
                for h in range(HC):
                    last = nc.scalar.activation(HT[:, h, :], PS[5 + h // 4][:, (h % 4) * P:(h % 4 + 1) * P], ACT.Relu,
                                                bias=B1[:, bass.ds(e * HC + h, 1)])
                last.then_inc(s_hT, 1)

            act.wait_ge(s_experts_known, 1)
            take_x(0, 0)
            take_x(1, 1)

            def experts(i):
                for u in range(2):
                    relu(2 * i + u)
                    take_x(2 * i + u + 2, u)

            experts(0)
            with act.Fori(1, (SLOT_TILES - 3) // 2) as i:
                experts(i)
            for t in range(SLOT_TILES - 3, SLOT_TILES):
                relu(t)
                if t + 2 < SLOT_TILES:
                    take_x(t + 2, t % 2)

        @block.gpsimd
        def _(pool):
            def spread(t, u):
                pool.wait_ge(s_k_hi, t + 1)
                free(pool, s_scored, t - 2)
                pool.sem_inc(s_pool_waits, 1)
                for h in range(GH):
                    last = pool.tensor_scalar(KXH[u][:, :, h, :], KH, CO[:, C_SLOTMASK + h:C_SLOTMASK + h + 1], 0.0, ALU.mult, ALU.add)
                last.then_inc(s_k_spread_high, 1)

            def spread_low(t, u):
                pool.wait_ge(s_k_low, t + 1)
                free(pool, s_scored, t - 2)
                pool.sem_inc(s_pool_waits, 1)
                for h in range(POOL_HEADS):
                    last = pool.tensor_scalar(KXL[u][:, :, h, :], KL, CO[:, C_SLOTMASK + h:C_SLOTMASK + h + 1], 0.0, ALU.mult, ALU.add)
                last.then_inc(s_k_spread_low, 1)

            def centre(t, u):
                pool.wait_ge(s_s_max, t + 1)
                pool.tensor_tensor(S[:, :, 0:NP], S[:, :, 0:NP], MX.unsqueeze(2).to_broadcast([P, G * GH, NP]),
                                   ALU.subtract).then_inc(s_s_centred, 1)

            def add_bias(q):
                pool.wait_ge(s_rows_in, 16)
                for t in tiles_of(q):
                    pool.wait_ge(s_copied, t + 1)
                    pool.tensor_tensor(X[:, t, :], X[:, t, :], ROWS[:, 0, :], ALU.add).then_inc(s_biased, 1)

            awv = AW.rearrange("p m (k g c) -> p m k g c", k=KC, g=G)

            def ternary(part):
                if part == 2:
                    pool.memset(PR, 0.0).then_inc(s_cleared, 1)
                    pool.wait_ge(s_weights_scaled, 4)
                    pool.tensor_scalar(AW, AW, -MAGIC, 1.0, ALU.add, ALU.min).then_inc(s_weights_cut, 1)
                if part == 3:
                    pool.wait_ge(s_weights_cut, 1)
                    for m in range(2):
                        for r in range(2):
                            for k in range(KC):
                                pool.tensor_scalar(TQK[:, k, m, :, r, :], awv[:, m, k, :, :], -1.0, 0.0, ALU.max, ALU.add)
                    for m, dst in ((2, TV), (3, TO[:, :, :])):
                        last = pool.tensor_scalar(dst, AW[:, m, :].rearrange("p (k c) -> p k c", k=KC), -1.0, 0.0, ALU.max, ALU.add)
                    last.then_inc(s_ternary, 1)

            def lay_ones(q):
                pool.wait_ge(s_embedded, TILES)
                for u in range(AB):
                    for j in range(BPT):
                        last = pool.tensor_copy(VX[u][:, j, :, GD:GD + GH],
                                                const(C_BMASK, BPT).unsqueeze(1).to_broadcast([P, G, GH]))
                last.then_inc(s_ones, 1)

            def to_int_range(q):
                pool.wait_ge(s_to_int, TILES // QT + q + 1)
                for t in tiles_of(q)[QT - POOL_TILES:]:
                    last = pool.tensor_scalar(X[:, t, :], X[:, t, :], SM[:, 10, t:t + 1], 0.0, ALU.mult, ALU.add)
                last.then_inc(s_to_int_pool, 1)

            follow(BEFORE_ATTENTION, {"p": add_bias, "w": ternary, "v": lay_ones})
            rounds(POOL_ROUND, {"spread": spread, "spread_low": spread_low, "centre": centre}, lambda n: pool.Fori(0, n))
            follow(AFTER_ATTENTION, {"g": to_int_range})

            for k in range(2):
                pool.wait_ge(s_gate_parts, 1)
                pool.wait_ge(s_tile_hot, k + 1)
                for f in range(FACTS - POOL_FACTS, FACTS):
                    pool.tensor_tensor(TILE1[:, f, k], TILE1[:, 0, k], FACT[:, f - 1, k, :].unsqueeze(2).to_broadcast([P, TILES, SLOT_TILES]),
                                       ALU.mult).then_inc(s_pool_facts_hot, 1)

            def gather(t, u):
                free(pool, s_xg_turned, t - 1)
                pool.sem_inc(s_pool_waits, 1)
                pool.tensor_copy(SIDX[:, 0, u:u + 1], TAKE[:, bass.ds(t, 1)]).then_inc(s_take_idx, 1)
                pool.wait_ge(s_take_idx, t + 1)
                pool.sem_inc(s_pool_waits, 1)
                pool.indirect_dma_start(XG[:, u, :], None, xs,
                                        bass.IndirectOffsetOnAxis(ap=SIDX[:, 0, u:u + 1], axis=0)).then_inc(s_xg_in[u], 16)

            def give(t, u):
                pool.tensor_copy(SIDX[:, 1, u:u + 1], GIVE[:, bass.ds(t, 1)]).then_inc(s_give_idx, 1)
                pool.wait_ge(s_give_idx, t + 1)
                pool.wait_ge(s_y_ready, t + 1)
                free(pool, s_y_added, 16 * t)
                pool.sem_inc(s_pool_waits, 1)
                pool.indirect_dma_start(out_rows, bass.IndirectOffsetOnAxis(ap=SIDX[:, 1, u:u + 1], axis=0), Y[:, u, :],
                                        None, bounds_check=B * NP - 1, oob_is_err=False,
                                        compute_op=ALU.add).then_inc(s_y_added, 16)

            pool.wait_ge(s_tables_known, 1)
            pool.wait_ge(s_rows_out, 16 * (TILES // QT))
            gather(0, 0)
            gather(1, 1)
            pool.wait_ge(s_residual_out, 16 * BPT)

            def experts(i):
                for u in range(2):
                    gather(2 * i + u + 2, u)
                    if not (isinstance(i, int) and i + u == 0):
                        give(2 * i + u - 1, 1 - u)

            experts(0)
            with pool.Fori(1, (SLOT_TILES - 3) // 2) as i:
                experts(i)
            for t in range(SLOT_TILES - 3, SLOT_TILES + 1):
                if t + 2 < SLOT_TILES:
                    gather(t + 2, t % 2)
                give(t - 1, (t - 1) % 2)
            pool.wait_ge(s_y_added, 16 * SLOT_TILES)

        @block.vector
        def _(dve):
            v = nc.vector
            step = Chain(dve, s_dve_step)
            MEAN, VAR = MV[:, :, 0], MV[:, :, 1]

            def col(i):
                return SM[:, i, :]

            means_asked = [0]

            def part(a, q):
                return a[:, QT * q:QT * (q + 1)]

            def moments(src, q, ask_mean=False):
                for t in tiles_of(q):
                    step.add(v.bn_stats(ST[:, t, :], src[:, t, :]))
                step.wait()
                for t in tiles_of(q):
                    step.add(v.bn_aggr(MV[:, t, :], ST[:, t, :]))
                step.wait()

            def ask_root(kind, q, var):
                v.tensor_scalar(part(col(2), q), var, EPS, None, ALU.add).then_inc(s_var[kind], 1)

            def inverse(kind, q, dst):
                c2, c3, c4, c5 = (part(col(i), q) for i in (2, 3, 4, 5))
                dve.wait_ge(s_var[kind], q + 1)
                dve.wait_ge(s_dev[kind], q + 1)
                step(v.reciprocal(c4, c3))
                step(v.scalar_tensor_tensor(c5, c4, -0.5, c4, ALU.mult, ALU.mult))
                step(v.tensor_tensor(c5, c5, c2, ALU.mult))
                step(v.scalar_tensor_tensor(part(col(dst), q), c5, 1.5, c4, ALU.add, ALU.mult))

            def factors(kind, q, mean):
                v.scalar_tensor_tensor(part(col(9), q), mean, -1.0, part(col(8), q), ALU.mult, ALU.mult).then_inc(s_factors[kind], 1)

            def ask_batch_mean(ins):
                ins.then_inc(s_part_sums, 1)
                means_asked[0] += 1
                return means_asked[0]

            asked = {}

            def to_int_factor(first, kind):
                def do(q):
                    dve.wait_ge(s_normed[kind], q + 1)
                    c5, c6, c8 = (part(col(i), q) for i in (5, 6, 8))
                    step(v.tensor_reduce(c5, X[:, QT * q:QT * (q + 1), :], AX.X, ALU.max, apply_absolute_value=True))
                    step(v.tensor_scalar(c5, c5, 1e-5, None, ALU.max))
                    step(v.reciprocal(c8, c5))
                    v.tensor_scalar(part(col(10), q), c8, 127.0, None, ALU.mult).then_inc(s_to_int, 1)
                    if first:
                        step.add(v.tensor_scalar(c6, c5, 1.0 / 127.0, AL[:, 1, 3:4], ALU.mult, ALU.mult))
                    else:
                        step.add(v.tensor_scalar(c6, c5, 1.0 / 127.0, None, ALU.mult))
                return do

            def round_int(first):
                def do(q):
                    x = X[:, QT * q:QT * (q + 1), :]
                    dve.wait_ge(s_to_int_done, first + q + 1)
                    if first:
                        dve.wait_ge(s_to_int_pool, q + 1)
                    step(v.tensor_scalar(x, x, -128.0, 127.0, ALU.max, ALU.min))
                    v.tensor_scalar(QI[:, QT * q:QT * (q + 1), :], x, MAGIC, -MAGIC, ALU.add, ALU.add).then_inc(s_quantised, 1)
                    if q == TILES // QT - 1:
                        dve.wait_ge(s_quantised, first + q + 1)
                return do

            def ternary(part):
                if part == 0:
                    dve.wait_ge(s_const_in, 16)
                    v.tensor_copy(IDB[:, :], const(C_IDENT, P)).then_inc(s_idb, 1)
                    dve.wait_ge(s_attn_w_in, 16)
                    v.tensor_reduce(AL[:, 0, :], AW, AX.X, ALU.add, apply_absolute_value=True).then_inc(s_abs_sums, 1)
                if part == 1:
                    dve.wait_ge(s_abs_total, 1)
                    step(v.tensor_scalar(AL[:, 1, :], PS[6][:, 0:4], 1.0 / (D * D), 1e-5, ALU.mult, ALU.max))
                    step(v.reciprocal(AL[:, 2, :], AL[:, 1, :]))
                    for m in range(4):
                        v.tensor_scalar(AW[:, m, :], AW[:, m, :], AL[:, 2, m:m + 1], MAGIC, ALU.mult, ALU.add).then_inc(s_weights_scaled, 1)
                    step.add(v.tensor_scalar(AL[:, 3, 0:1], AL[:, 1, 0:1], AL[:, 1, 1:2], HD ** -0.5, ALU.mult, ALU.mult))

            def token_moments(q):
                dve.wait_ge(s_biased, QT * (q + 1))
                moments(X, q)
                ask_root("token", q, part(VAR, q))
                for t in tiles_of(q):
                    step.add(v.scalar_tensor_tensor(X[:, t, :], X[:, t, :], MV[:, t, 0:1], ROWS[:, 1, :], ALU.subtract, ALU.mult))

            def tokens(q):
                inverse("token", q, 8)
                for t in tiles_of(q):
                    step.add(v.scalar_tensor_tensor(H[:, t, :], X[:, t, :], SM[:, 8, t:t + 1], ROWS[:, 2, :], ALU.mult, ALU.add))

            def row_moments(q):
                step.wait()
                moments(H, q)
                ask_root("row", q, part(VAR, q))

            def normed_squares(q):
                inverse("row", q, 7)
                step(v.tensor_tensor(part(col(0), q), part(VAR, q), part(col(7), q), ALU.mult))
                asked[q] = ask_batch_mean(v.tensor_tensor(part(col(0), q), part(col(0), q), part(col(7), q), ALU.mult))

            def batch_root(kind):
                def do(q):
                    dve.wait_ge(s_batch_means, asked[q])
                    ask_root(kind, q, psM[q])
                return do

            def row_and_batch_factors(q):
                inverse("batch", q, 8)
                step(v.tensor_tensor(part(col(8), q), part(col(8), q), part(col(7), q), ALU.mult))
                factors("batch", q, part(MEAN, q))

            def scale_layouts(q):
                step.wait()
                v.tensor_tensor(DV, scale.to_broadcast([P, TILES, BPT]),
                                const(C_BMASK, BPT).unsqueeze(1).to_broadcast([P, TILES, BPT]), ALU.mult).then_inc(s_scale_diag, 1)
                v.tensor_tensor(SIG, scale.to_broadcast([P, TILES, PADN]),
                                const(C_DMASK, PADN).unsqueeze(1).to_broadcast([P, TILES, PADN]), ALU.mult).then_inc(s_scale_diag, 1)

            scale = SM[:, 6, :].unsqueeze(2)
            dve.wait_ge(s_rows_in, 16)
            follow(BEFORE_ATTENTION, {"a": token_moments, "w": ternary, "b": tokens, "c": row_moments, "d": normed_squares,
                                      "e": batch_root("batch"), "f": row_and_batch_factors, "g": to_int_factor(0, "batch"),
                                      "s": scale_layouts, "h": round_int(0)})
            dve.wait_ge(s_scale_rep, 2)
            step(v.tensor_scalar(SREP, PS[6][:, 0:TILES * BPT], AL[:, 1, 2:3], None, ALU.mult))
            v.scalar_tensor_tensor(SIG, PS[5][:, :].rearrange("p (t n) -> p t n", t=TILES), AL[:, 3, 0:1],
                                   scale.to_broadcast([P, TILES, PADN]), ALU.mult, ALU.mult).then_inc(s_scales_read, 1)
            dve.wait_ge(s_scales_read, 1)

            def low_q(t, u):
                dve.wait_ge(s_q_hi, t + 1)
                v.tensor_tensor(QS[u][GD:P], psQ[GD:P], QS[u][GD:P], ALU.subtract).then_inc(s_q_split, 1)

            def low_k(t, u):
                dve.wait_ge(s_k_hi, t + 1)
                free(dve, s_k_spread, t)
                free(dve, s_k_spread_low, t)
                v.tensor_tensor(KL, psK, KH, ALU.subtract).then_inc(s_k_low, 1)
                dve.wait_ge(s_k_low, t + 1)
                free(dve, s_scored, t - 2)
                for h in range(POOL_HEADS, GH):
                    last = v.tensor_scalar(KXL[u][:, :, h, :], KL, CO[:, C_SLOTMASK + h:C_SLOTMASK + h + 1], None, ALU.mult)
                last.then_inc(s_k_spread, 1)

            def scale_scores(t, u):
                dve.wait_ge(s_scored, t + 1)
                free(dve, s_probs, t)
                v.tensor_tensor(S, psS[:, :].rearrange("p (h n) -> p h n", n=PADN),
                                SIG[:, bass.ds(t, 1), :].to_broadcast([P, G * GH, PADN]), ALU.mult).then_inc(s_s_scaled, 1)
                dve.wait_ge(s_s_scaled, t + 1)
                v.tensor_reduce(MX, S[:, :, 0:NP], AX.X, ALU.max).then_inc(s_s_max, 1)

            def attend(t, u):
                dve.wait_ge(s_mixed, t + 1)
                step(v.reciprocal(RS.rearrange("p (g h) -> p g h", g=G), psA[:, :, GD:GD + GH]))
                v.tensor_tensor(X[:, t, :].rearrange("p (g h d) -> p g h d", g=G, h=GH),
                                psA[:, :, 0:GD].rearrange("p g (h d) -> p g h d", h=GH),
                                RS.rearrange("p (g h) -> p g h", g=G).unsqueeze(3).to_broadcast([P, G, GH, HD]),
                                ALU.mult).then_inc(s_attended, 1)
                dve.wait_ge(s_attended, t + 1)

            def spread_v(t, u):
                dve.wait_ge(s_v_made, t + 1)
                free(dve, s_mixed, t - 2)
                for j in range(BPT):
                    last = v.scalar_tensor_tensor(
                        VX[u][:, j, :, 0:GD], psV[j].rearrange("p (g c) -> p g c", g=G), SREP[:, bass.ds(t * BPT + j, 1)],
                        const(C_HMASK, GD).unsqueeze(1).to_broadcast([P, G, GD]), ALU.mult, ALU.mult)
                last.then_inc(s_v_spread, 1)

            def out_mean(q):
                moments(X, q)
                asked[q] = ask_batch_mean(v.tensor_copy(part(col(0), q), part(MEAN, q)))

            def drain(q):
                if q in DRAIN:
                    dve.wait_ge(s_attended, QT * (q + 1))
                    out_mean(q)

            step.wait()
            rounds(DVE_ROUND, {"low_q": low_q, "low_k": low_k, "spread_v": spread_v, "scale": scale_scores, "attend": attend},
                   lambda n: step.loop(0, n, AB), drain)

            def out_squares(q):
                dve.wait_ge(s_batch_means, asked[q])
                c5, c7 = part(col(5), q), part(col(7), q)
                step(v.tensor_copy(c7, psM[q]))
                step(v.tensor_tensor(c5, part(MEAN, q), c7, ALU.subtract))
                step(v.tensor_tensor(c5, c5, c5, ALU.mult))
                asked[q] = ask_batch_mean(v.tensor_tensor(part(col(1), q), c5, part(VAR, q), ALU.add))

            def out_factors(q):
                inverse("batch2", q, 8)
                factors("batch2", q, part(col(7), q))

            def add_attention(q):
                for t in tiles_of(q):
                    dve.wait_ge(s_o_made, t + 1)
                    v.scalar_tensor_tensor(H[:, t, :], psO[t % 2], SM[:, 6, t:t + 1], H[:, t, :], ALU.mult, ALU.add).then_inc(s_h_new, 1)
                dve.wait_ge(s_h_new, QT * (q + 1))
                moments(H, q)
                ask_root("row2", q, part(VAR, q))

            def norm_rows(q):
                inverse("row2", q, 8)
                for t in tiles_of(q):
                    last = v.tensor_scalar(X[:, t, :], H[:, t, :], MV[:, t, 0:1], SM[:, 8, t:t + 1], ALU.subtract, ALU.mult)
                last.then_inc(s_normed["row2"], 1)

            follow(AFTER_ATTENTION, {"c": lambda q: q in DRAIN or out_mean(q), "d": out_squares, "e": batch_root("batch2"), "f": out_factors,
                                     "g": to_int_factor(TILES // QT, "batch2"), "h": round_int(TILES // QT),
                                     "o": add_attention, "x": norm_rows})
            dve.wait_ge(s_misc_in, 48)
            dve.wait_ge(s_logits_made, TILES)
            step(v.tensor_tensor(R[:, 1, :, :], psL[:, 0:TILES * E].rearrange("p (t e) -> p t e", e=E),
                                 GB[:, :].unsqueeze(1).to_broadcast([P, TILES, E]), ALU.add))

            def r(i):
                return R[:, i, :, :]

            def wide(i):
                return SM[:, i, :].unsqueeze(2).to_broadcast([P, TILES, E])

            down = const(C_DOWN, E).unsqueeze(1).to_broadcast([P, TILES, E])
            step(v.tensor_reduce(col(0), r(1), AX.X, ALU.max))
            v.tensor_tensor(r(2), r(1), wide(0), ALU.subtract).then_inc(s_logits_centred, 1)
            dve.wait_ge(s_logits_exp, 1)
            dve.wait_ge(s_exp_loaded, 1)
            step(v.tensor_reduce(col(1), r(1), AX.X, ALU.add))
            step(v.reciprocal(col(1), col(1)))
            for k in range(2):
                step(v.tensor_reduce(col(0), r(1), AX.X, ALU.max))
                step.add(v.tensor_tensor(GATE[:, k, :], col(0), col(1), ALU.mult))
                step(v.tensor_tensor(r(2), r(1), wide(0), ALU.is_ge))
                step(v.tensor_tensor(r(2), r(2), down, ALU.mult))
                step(v.tensor_reduce(col(2), r(2), AX.X, ALU.max))
                step(v.tensor_tensor(r(3 + k), down, wide(2), ALU.is_equal))
                if k == 0:
                    step(v.scalar_tensor_tensor(r(1), r(3), -2.0, r(1), ALU.mult, ALU.add))
            step(v.tensor_tensor(r(0), r(3), r(4), ALU.add))
            v.tensor_scalar(r(0), r(0), CO[:, C_VALID:C_VALID + 1], None, ALU.mult).then_inc(s_picks, 1)
            step(v.tensor_copy(FACT[:, 0:2], const(C_TOKEN, 4 * TILES).rearrange("p (f k t) -> p f k t", f=2, k=2)))
            step(v.tensor_copy(FACT[:, 2], GATE[:, :, :]))
            step(v.tensor_tensor(REST[:, :, :], GATE[:, :, :], FACT[:, 2], ALU.subtract))
            step(v.tensor_copy(FACT[:, 3], REST[:, :, :]))
            v.tensor_tensor(FACT[:, 4], REST[:, :, :], FACT[:, 3], ALU.subtract).then_inc(s_gate_parts, 1)
            dve.wait_ge(s_ranked, 2)
            step(v.tensor_copy(r(5), PS[2][:, 0:TILES * E].rearrange("p (t e) -> p t e", e=E)))
            a, b = 5, 6
            for d in (1, 2, 4, 8):
                step.add(v.tensor_copy(R[:, b, 0:d, :], R[:, a, 0:d, :]))
                step(v.tensor_tensor(R[:, b, d:, :], R[:, a, d:, :], R[:, a, 0:TILES - d, :], ALU.add))
                a, b = b, a
            count = R[:, a, TILES - 1, :]
            cum = R[:, 7, 0, :]
            cum2 = R[:, 7, 1, :]
            step(v.tensor_scalar(cum, count, 1.0 / P, (P - 1) / P - (P - 1) / (2 * P), ALU.mult, ALU.add))
            step(v.tensor_scalar(cum, cum, MAGIC, -MAGIC, ALU.add, ALU.add))
            step(v.tensor_copy(R[:, 7, 2, :], cum))
            x, y = 0, 1
            for d in (1, 2, 4):
                step.add(v.tensor_copy(R[:, 7, y, 0:d], R[:, 7, x, 0:d]))
                step(v.tensor_tensor(R[:, 7, y, d:], R[:, 7, x, d:], R[:, 7, x, 0:E - d], ALU.add))
                x, y = y, x
            step(v.tensor_tensor(R[:, 7, 2, :], R[:, 7, x, :], R[:, 7, 2, :], ALU.subtract))
            step(v.tensor_scalar(R[:, 7, 2, :], R[:, 7, 2, :], float(P), None, ALU.mult))
            step(v.tensor_tensor(ET[:, :, :], const(C_TILE, SLOT_TILES).unsqueeze(2).to_broadcast([P, SLOT_TILES, E]),
                                 R[:, 7, x:x + 1, :].to_broadcast([P, SLOT_TILES, E]), ALU.is_ge))
            step(v.tensor_reduce(EF[:, :], ET[:, :, :], AX.X, ALU.add))
            v.tensor_scalar(EI[:, :], EF[:, :], float(E - 1), None, ALU.min).then_inc(s_experts_known, 1)
            step(v.tensor_tensor(r(8), PS[1][:, 0:TILES * E].rearrange("p (t e) -> p t e", e=E),
                                 R[:, 7, 2:3, :].to_broadcast([P, TILES, E]), ALU.add))
            step(v.tensor_tensor(R[:, 8, 1:, :], R[:, 8, 1:, :], R[:, a, 0:TILES - 1, :], ALU.add))
            for k in range(2):
                step(v.tensor_tensor(r(9), r(8), r(3 + k), ALU.mult))
                step(v.tensor_reduce(SLOT[:, k, :], r(9), AX.X, ALU.add))
            step(v.tensor_scalar(SLOT[:, :, :], SLOT[:, :, :], 1.0, CO[:, C_VALID:C_VALID + 1], ALU.add, ALU.mult))
            step(v.tensor_scalar(SLOT[:, :, :], SLOT[:, :, :], -1.0, None, ALU.add))
            step(v.tensor_scalar(SLOTT[:, :, :], SLOT[:, :, :], 1.0 / P, -(P - 1) / (2 * P), ALU.mult, ALU.add))
            step(v.tensor_scalar(SLOTT[:, :, :], SLOTT[:, :, :], MAGIC, -MAGIC, ALU.add, ALU.add))
            step(v.scalar_tensor_tensor(SLOT[:, :, :], SLOTT[:, :, :], -float(P), SLOT[:, :, :], ALU.mult, ALU.add))
            dve.wait_ge(s_rows_out, 16 * (TILES // QT))
            tiles_hot, rows_hot = [P, TILES, SLOT_TILES], [P, TILES, P]
            for k in range(2):
                v.tensor_tensor(TILE1[:, 0, k], SLOTT[:, k, :].unsqueeze(2).to_broadcast(tiles_hot),
                                const(C_TILE, SLOT_TILES).unsqueeze(1).to_broadcast(tiles_hot), ALU.is_equal).then_inc(s_tile_hot, 1)
                v.tensor_tensor(ROW1[:, k], SLOT[:, k, :].unsqueeze(2).to_broadcast(rows_hot),
                                const(C_ROW, P).unsqueeze(1).to_broadcast(rows_hot), ALU.is_equal).then_inc(s_row_hot, 1)
                dve.wait_ge(s_tile_hot, k + 1)
                for f in range(1, FACTS - POOL_FACTS):
                    v.tensor_tensor(TILE1[:, f, k], TILE1[:, 0, k], FACT[:, f - 1, k, :].unsqueeze(2).to_broadcast(tiles_hot),
                                    ALU.mult).then_inc(s_facts_hot, 1)
            dve.wait_ge(s_tables_made, 1)
            step(v.tensor_copy(ET[:, :, 0:FACTS].rearrange("p s f -> p f s"),
                               PS[3][:, 0:FACTS * SLOT_TILES].rearrange("p (f s) -> p f s", f=FACTS)))
            step.add(v.scalar_tensor_tensor(TAKE[:, :], ET[:, :, 1], float(PADN), ET[:, :, 2], ALU.mult, ALU.add))
            step.add(v.tensor_tensor(SGATE[:, :], ET[:, :, 3], ET[:, :, 4], ALU.add))
            step(v.scalar_tensor_tensor(EF[:, :], ET[:, :, 1], float(NP), ET[:, :, 2], ALU.mult, ALU.add))
            step.add(v.tensor_tensor(SGATE[:, :], SGATE[:, :], ET[:, :, 5], ALU.add))
            step(v.tensor_scalar(EF[:, :], EF[:, :], float(BEYOND), None, ALU.add))
            v.scalar_tensor_tensor(GIVE[:, :], ET[:, :, 0], -float(BEYOND), EF[:, :], ALU.mult, ALU.add).then_inc(s_tables_known, 1)
            dve.wait_ge(s_tables_known, 1)

            def take_hidden(t, u):
                dve.wait_ge(s_hidden, t + 1)
                free(dve, s_h_turned, t - 1)
                for half in range(2):
                    last = v.tensor_copy(HP[:, u, half * 512:(half + 1) * 512], PS[1 + 2 * u + half][:, :])
                last.then_inc(s_hp_ready, 1)

            def take_y(t, u, i):
                e = dve.value_load(EI[0:1, bass.ds(t, 1)], min_val=0, max_val=E - 1)
                dve.wait_ge(s_y_made, t + 1)
                free(dve, s_y_added, 16 * (t - 1))
                v.tensor_tensor(Y[:, u, :], PS[7][:, 0:D], B2[:, e, :], ALU.add).then_inc(s_y_biased, 1)
                dve.wait_ge(s_y_biased, t + 1)
                v.tensor_scalar(Y[:, u, :], Y[:, u, :], SGATE[:, bass.ds(t, 1)], None, ALU.mult).then_inc(s_y_ready, 1)

            dve.wait_ge(s_experts_known, 1)
            take_hidden(0, 0)

            def experts(i):
                for u in range(2):
                    take_hidden(2 * i + u + 1, 1 - u)
                    take_y(2 * i + u, u, i)

            experts(0)
            with dve.Fori(1, (SLOT_TILES - 3) // 2) as i:
                experts(i)
            for t in range(SLOT_TILES - 3, SLOT_TILES):
                if t + 1 < SLOT_TILES:
                    take_hidden(t + 1, (t + 1) % 2)
                take_y(t, t % 2, t // 2)


def kernel(x, L0_tok_W, L0_tok_b, L0_tok_gamma, L0_tok_beta, L0_attn_w_q, L0_attn_w_k, L0_attn_w_v, L0_attn_w_o,
           L0_ffn_gate_w, L0_ffn_gate_b, L0_ffn_w1, L0_ffn_b1, L0_ffn_w2, L0_ffn_b2):
    import concourse.bacc as bacc
    from concourse.bass_utils import run_bass_kernel_spmd

    def wide(a):
        return np.broadcast_to(a, (P,) + a.shape)

    x = np.asarray(x)
    pixels = np.zeros((B, MELS, PF, PADN), x.dtype)
    for f in range(PF):
        pixels[:, :, f, :NP] = x[:, :, f:f + HOP * (NP - 1) + 1:HOP]
    xp = pixels.reshape(TILES, BPT, 5, P, PADN).transpose(0, 3, 2, 1, 4).reshape(TILES, P, 5, P)
    wt = np.asarray(L0_tok_W).reshape(5, P, D).transpose(1, 0, 2)
    attn = [np.asarray(a).T.reshape(KC, P, D).transpose(1, 0, 2).reshape(P, KC * D)
            for a in (L0_attn_w_q, L0_attn_w_k, L0_attn_w_v, L0_attn_w_o)]
    arrays = {
        "xp": xp, "wt": wt,
        "rows": wide(np.stack([np.asarray(a) for a in (L0_tok_b, L0_tok_gamma, L0_tok_beta)])),
        "attn_w": np.stack(attn, 1),
        "gate_w": np.asarray(L0_ffn_gate_w).T.reshape(KC, P, E).transpose(1, 0, 2),
        "gate_b": wide(np.asarray(L0_ffn_gate_b)),
        "w1": np.asarray(L0_ffn_w1),
        "b1": np.asarray(L0_ffn_b1).reshape(E * HC, P).T,
        "w2": np.asarray(L0_ffn_w2),
        "b2": wide(np.asarray(L0_ffn_b2)),
        "const": constants(),
    }
    arrays = {f"in_{k}": np.ascontiguousarray(a) for k, a in arrays.items()}
    nc = bacc.Bacc("TRN2", target_bir_lowering=False, num_devices=1)
    args = [nc.dram_tensor(k, a.shape, mybir.dt.from_np(a.dtype), kind="ExternalInput").ap() for k, a in arrays.items()]
    args.append(nc.dram_tensor("out", (B, NP, D), mybir.dt.float32, kind="ExternalOutput").ap())
    build(nc, *args)
    r = run_bass_kernel_spmd(nc, [arrays], core_ids=[0])
    return r.results[0]["out"]
```
